# Optimizing a Trainium2 kernel written in Bass

```python
import numpy as np
import jax
import jax.numpy as jnp

def _softmax(x, axis=-1):
    return jax.nn.softmax(x, axis=axis)

def _gelu(x):
    return jax.nn.gelu(x, approximate=True)

def _silu(x):
    return jax.nn.silu(x)

def _sigmoid(x):
    return jax.nn.sigmoid(x)

def _layernorm(x, axis=-1, eps=1e-05):
    m = jnp.mean(x, axis=axis, keepdims=True)
    v = jnp.var(x, axis=axis, keepdims=True)
    return (x - m) / jnp.sqrt(v + eps)

def _scatter_add(tgt, idx, src, axis=0):
    return tgt.at[idx].add(src)

def _segment_sum(src, seg, n):
    return jax.ops.segment_sum(src, seg, n)
kernel_name = 'mk_gnn_ffn_d4_gnn_r32_24a8f5'

def setup_inputs(seed: int=0):
    np.random.seed(seed)
    _w = jnp.asarray

    def _rec_inputs():
        import jax
        import jax.numpy as jnp
        _gk = jax.random.key(seed)
        x = -0.0003713 + 1 * jax.random.normal(jax.random.fold_in(_gk, 1), (3125, 256), jnp.float32)
        src = jax.random.randint(jax.random.fold_in(_gk, 2), (50000,), 0, 3125, jnp.int32)
        dst = jnp.minimum((3125 * jax.random.uniform(jax.random.fold_in(_gk, 3), (50000,)) ** 2.0).astype(jnp.int32), 99999)
        _o = jnp.argsort(dst, stable=True)
        src = src[_o]
        dst = dst[_o]
        edge_attr_64 = -9.77346e-05 + 0.999888 * jax.random.normal(jax.random.fold_in(_gk, 12), (50000, 64), jnp.float32)
        return (x, src, dst, edge_attr_64)
    x, src, dst, edge_attr_64 = _rec_inputs()

    def _L0_gnn_setup():
        import jax, jax.numpy as jnp
        import numpy as np
        N_NODES = 50000
        N_EDGES = 25000
        IN_DIM = 256
        E_DIM = 64
        N_HEADS = 8
        OUT_DIM = 32
        NEG_SLOPE = 0.2
        key = jax.random.key(seed)
        ks = jax.random.split(key, 10)
        return {'feat': jax.random.normal(ks[0], (N_NODES, IN_DIM), dtype=jnp.float32), 'edge_attr': jax.random.normal(ks[1], (N_EDGES, E_DIM), dtype=jnp.float32), 'src': jax.random.randint(ks[2], (N_EDGES,), 0, N_NODES, dtype=jnp.int32), 'dst': jax.random.randint(ks[3], (N_EDGES,), 0, N_NODES, dtype=jnp.int32), 'W_fc': jax.random.normal(ks[4], (IN_DIM, N_HEADS * OUT_DIM), dtype=jnp.float32) * (1.0 / np.sqrt(IN_DIM)), 'W_e': jax.random.normal(ks[5], (E_DIM, N_HEADS * OUT_DIM), dtype=jnp.float32) * (1.0 / np.sqrt(E_DIM)), 'attn_h': jax.random.normal(ks[6], (N_HEADS, OUT_DIM), dtype=jnp.float32) * 0.1, 'attn_e': jax.random.normal(ks[7], (N_HEADS, OUT_DIM), dtype=jnp.float32) * 0.1, 'attn_t': jax.random.normal(ks[8], (N_HEADS, OUT_DIM), dtype=jnp.float32) * 0.1, 'bias': jnp.zeros((N_HEADS, OUT_DIM), dtype=jnp.float32)}
    _L0_gnn_all = _L0_gnn_setup()
    _L0_gnn_in = {k: v for k, v in _L0_gnn_all.items() if k in ('W_fc', 'W_e', 'attn_h', 'attn_e', 'attn_t', 'bias')}
    del _L0_gnn_all

    def _L0_ffn_setup():
        import jax, jax.numpy as jnp
        import numpy as np
        BN_EPS = 0.001

        def _bn(h, g, b, m, v):
            return g * (h - m) * jax.lax.rsqrt(v + BN_EPS) + b
        key = jax.random.key(seed)
        ks = jax.random.split(key, 8)
        B, F, Df = (256, 64, 256)
        E, H, D = (8, 256, 256)
        s1 = 1.0 / np.sqrt(Df)
        s2 = 1.0 / np.sqrt(H)
        return {'x': jax.random.normal(ks[0], (B, F, Df), jnp.float32), 'Wr': jax.random.normal(ks[1], (Df, E), jnp.float32) * s1, 'br': jnp.zeros((E,), jnp.float32), 'W1': jax.random.normal(ks[2], (E, Df, H), jnp.float32) * s1, 'b1': jnp.zeros((E, H), jnp.float32), 'g1': jnp.ones((E, H), jnp.float32), 'be1': jnp.zeros((E, H), jnp.float32), 'm1': jnp.zeros((E, H), jnp.float32), 'v1': jnp.ones((E, H), jnp.float32), 'W2': jax.random.normal(ks[3], (E, H, H), jnp.float32) * s2, 'b2': jnp.zeros((E, H), jnp.float32), 'g2': jnp.ones((E, H), jnp.float32), 'be2': jnp.zeros((E, H), jnp.float32), 'm2': jnp.zeros((E, H), jnp.float32), 'v2': jnp.ones((E, H), jnp.float32), 'Wo': jax.random.normal(ks[4], (E, H, D), jnp.float32) * s2, 'bo': jnp.zeros((E, D), jnp.float32)}
    _L0_ffn_all = _L0_ffn_setup()
    _L0_ffn_in = {k: v for k, v in _L0_ffn_all.items() if k in ('Wr', 'br', 'W1', 'b1', 'g1', 'be1', 'm1', 'v1', 'W2', 'b2', 'g2', 'be2', 'm2', 'v2', 'Wo', 'bo')}
    del _L0_ffn_all

    def _L1_gnn_setup():
        import jax, jax.numpy as jnp
        import numpy as np
        N_NODES = 10000
        N_EDGES = 10000
        D = 256
        L = 3
        BN_EPS = 1e-05

        def _segment_softmax(logits, seg, num_segments):
            m = jax.ops.segment_max(logits, seg, num_segments=num_segments)
            e = jnp.exp(logits - m[seg])
            s = jax.ops.segment_sum(e, seg, num_segments=num_segments)
            return e / s[seg]
        key = jax.random.key(seed)
        ks = jax.random.split(key, 20)
        scale = 1.0 / np.sqrt(D)
        inp = {'x': jax.random.normal(ks[0], (N_NODES, D), dtype=jnp.float32), 'edge_index': jax.random.randint(ks[1], (2, N_EDGES), 0, N_NODES, dtype=jnp.int64), 'Wq': jax.random.normal(ks[2], (D, D), jnp.float32) * scale, 'bq': jnp.zeros((D,), jnp.float32), 'Wk': jax.random.normal(ks[3], (D, D), jnp.float32) * scale, 'bk': jnp.zeros((D,), jnp.float32), 'Wv': jax.random.normal(ks[4], (D, D), jnp.float32) * scale, 'bv': jnp.zeros((D,), jnp.float32), 'Ws': jax.random.normal(ks[5], (D, D), jnp.float32) * scale, 'bs': jnp.zeros((D,), jnp.float32), 'Wl': jax.random.normal(ks[6], (L, D, D), jnp.float32) * scale, 'bl': jnp.zeros((L, D), jnp.float32), 'Wr': jax.random.normal(ks[7], (L, D, D), jnp.float32) * scale, 'gamma': jnp.ones((L, D), jnp.float32) + 0.1 * jax.random.normal(ks[8], (L, D), jnp.float32), 'beta': 0.1 * jax.random.normal(ks[9], (L, D), jnp.float32), 'alpha_res': jnp.asarray(0.5, jnp.float32)}
        return inp
    _L1_gnn_all = _L1_gnn_setup()
    _L1_gnn_in = {k: v for k, v in _L1_gnn_all.items() if k in ('Wq', 'bq', 'Wk', 'bk', 'Wv', 'bv', 'Ws', 'bs', 'Wl', 'bl', 'Wr', 'gamma', 'beta', 'alpha_res')}
    del _L1_gnn_all

    def _L1_ffn_setup():
        import jax, jax.numpy as jnp
        import numpy as np
        D_MODEL = 256
        EXPERT_DIM = 512
        NUM_EXPERTS = 8
        TOP_K = 2
        SEQ_LEN = 64
        BATCH = 2
        key = jax.random.key(seed)
        ks = jax.random.split(key, 8)
        s = 0.02
        x = jax.random.normal(ks[0], (SEQ_LEN, BATCH, D_MODEL), dtype=jnp.float32)
        Wg = jax.random.normal(ks[1], (D_MODEL, NUM_EXPERTS), dtype=jnp.float32) * s
        bg = jax.random.normal(ks[2], (NUM_EXPERTS,), dtype=jnp.float32) * s
        bias = jnp.zeros((NUM_EXPERTS,), dtype=jnp.float32)
        W1 = jax.random.normal(ks[3], (NUM_EXPERTS, D_MODEL, EXPERT_DIM), dtype=jnp.float32) * s
        b1 = jax.random.normal(ks[4], (NUM_EXPERTS, EXPERT_DIM), dtype=jnp.float32) * s
        W2 = jax.random.normal(ks[5], (NUM_EXPERTS, EXPERT_DIM, D_MODEL), dtype=jnp.float32) * s
        b2 = jax.random.normal(ks[6], (NUM_EXPERTS, D_MODEL), dtype=jnp.float32) * s
        return {'x': x, 'Wg': Wg, 'bg': bg, 'bias': bias, 'W1': W1, 'b1': b1, 'W2': W2, 'b2': b2}
    _L1_ffn_all = _L1_ffn_setup()
    _L1_ffn_in = {k: v for k, v in _L1_ffn_all.items() if k in ('Wg', 'bg', 'bias', 'W1', 'b1', 'W2', 'b2')}
    del _L1_ffn_all

    def _L2_gnn_setup():
        import jax, jax.numpy as jnp
        import numpy as np
        N_NODES = 50000
        N_EDGES = 25000
        IN_DIM = 256
        HEADS = 4
        HEAD_DIM = 64
        NEG_SLOPE = 0.2
        key = jax.random.key(seed)
        k1, k2, k3, k4, k5 = jax.random.split(key, 5)
        x = jax.random.normal(k1, (N_NODES, IN_DIM), dtype=jnp.float32)
        edge_index = jax.random.randint(k2, (2, N_EDGES), 0, N_NODES, dtype=jnp.int64)
        W = jax.random.normal(k3, (IN_DIM, HEADS * HEAD_DIM), dtype=jnp.float32) * (1.0 / np.sqrt(IN_DIM))
        att_src = jax.random.normal(k4, (HEADS, HEAD_DIM), dtype=jnp.float32) * (1.0 / np.sqrt(HEAD_DIM))
        att_dst = jax.random.normal(k5, (HEADS, HEAD_DIM), dtype=jnp.float32) * (1.0 / np.sqrt(HEAD_DIM))
        bias = jnp.zeros((HEADS * HEAD_DIM,), dtype=jnp.float32)
        return {'x': x, 'edge_index': edge_index, 'W': W, 'att_src': att_src, 'att_dst': att_dst, 'bias': bias}
    _L2_gnn_all = _L2_gnn_setup()
    _L2_gnn_in = {k: v for k, v in _L2_gnn_all.items() if k in ('W', 'att_src', 'att_dst', 'bias')}
    del _L2_gnn_all

    def _L2_ffn_setup():
        import jax, jax.numpy as jnp
        import numpy as np
        NUM_EXPERTS = 8
        TOP_K = 2
        B, S, D = (8, 256, 256)

        def _moe(tokens, router_w, w1, b1, w2, b2):
            N = tokens.shape[0]
            E = router_w.shape[0]
            logits = tokens.astype(jnp.float32) @ router_w.astype(jnp.float32).T
            probs = jax.nn.softmax(logits, axis=-1)
            rw, re = jax.lax.top_k(probs, TOP_K)
            if TOP_K > 1:
                rw = rw / jnp.maximum(rw.sum(-1, keepdims=True), 1e-12)
            rw = rw.astype(tokens.dtype)
            combine = jnp.zeros((N, E), tokens.dtype).at[jnp.arange(N)[:, None], re].set(rw)
            out = tokens
            for e in range(E):
                h = jax.nn.gelu(tokens @ w1[e] + b1[e], approximate=False)
                y = h @ w2[e] + b2[e]
                out = out + combine[:, e:e + 1] * y
            return out
        key = jax.random.key(seed)
        ks = jax.random.split(key, 4)
        scale = 1.0 / np.sqrt(D).astype(np.float32)
        return {'input_embeddings': jax.random.normal(ks[0], (B, S, D), jnp.float32), 'router_w': jax.random.normal(ks[1], (NUM_EXPERTS, D), jnp.float32) * scale, 'w1': jax.random.normal(ks[2], (NUM_EXPERTS, D, D), jnp.float32) * scale, 'b1': jnp.zeros((NUM_EXPERTS, D), jnp.float32), 'w2': jax.random.normal(ks[3], (NUM_EXPERTS, D, D), jnp.float32) * scale, 'b2': jnp.zeros((NUM_EXPERTS, D), jnp.float32)}
    _L2_ffn_all = _L2_ffn_setup()
    _L2_ffn_in = {k: v for k, v in _L2_ffn_all.items() if k in ('router_w', 'w1', 'b1', 'w2', 'b2')}
    del _L2_ffn_all

    def _L3_gnn_setup():
        import jax, jax.numpy as jnp
        import numpy as np
        N_NODES = 50000
        N_EDGES = 25000
        FEAT = 256
        EDIM = 64
        OUT = 256
        key = jax.random.key(seed)
        ks = jax.random.split(key, 12)
        s_in = 1.0 / np.sqrt(FEAT)
        s_u = 1.0 / np.sqrt(OUT + EDIM)
        s_ro = 1.0 / np.sqrt(OUT)
        return {'x': jax.random.normal(ks[0], (N_NODES, FEAT), jnp.float32), 'he': jax.random.normal(ks[1], (N_EDGES, EDIM), jnp.float32), 'src': jax.random.randint(ks[2], (N_EDGES,), 0, N_NODES, jnp.int32), 'dst': jax.random.randint(ks[3], (N_EDGES,), 0, N_NODES, jnp.int32), 'W_in': jax.random.normal(ks[4], (FEAT, OUT), jnp.float32) * s_in, 'b_in': jnp.zeros((OUT,), jnp.float32), 'W_u0': jax.random.normal(ks[5], (OUT + EDIM, OUT), jnp.float32) * s_u, 'b_u0': jnp.zeros((OUT,), jnp.float32), 'W_u1': jax.random.normal(ks[6], (OUT + EDIM, OUT), jnp.float32) * s_u, 'b_u1': jnp.zeros((OUT,), jnp.float32), 'W_ro': jax.random.normal(ks[7], (OUT, OUT), jnp.float32) * s_ro, 'b_ro': jnp.zeros((OUT,), jnp.float32)}
    _L3_gnn_all = _L3_gnn_setup()
    _L3_gnn_in = {k: v for k, v in _L3_gnn_all.items() if k in ('W_in', 'b_in', 'W_u0', 'b_u0', 'W_u1', 'b_u1', 'W_ro', 'b_ro')}
    del _L3_gnn_all

    def _L3_ffn_setup():
        import jax, jax.numpy as jnp
        import numpy as np
        DIM = 256
        H = 8
        D = 64
        G = 64
        INNER = H * D
        SCALE = D ** (-0.5)
        key = jax.random.key(seed)
        ks = jax.random.split(key, 12)
        B, N = (4, 512)
        x = jax.random.normal(ks[0], (B, N, DIM), dtype=jnp.float32)
        s = lambda fan_in: 1.0 / np.sqrt(fan_in)
        W_fx = jax.random.normal(ks[1], (DIM, INNER), dtype=jnp.float32) * s(DIM)
        b_fx = jnp.zeros((INNER,), dtype=jnp.float32)
        W_x = jax.random.normal(ks[2], (DIM, INNER), dtype=jnp.float32) * s(DIM)
        b_x = jnp.zeros((INNER,), dtype=jnp.float32)
        A = jax.random.normal(ks[3], (G, D), dtype=jnp.float32)
        Q, _ = jnp.linalg.qr(A.T)
        W_slice = Q[:, :G].astype(jnp.float32)
        b_slice = jnp.zeros((G,), dtype=jnp.float32)
        W_q = jax.random.normal(ks[4], (D, D), dtype=jnp.float32) * s(D)
        W_k = jax.random.normal(ks[5], (D, D), dtype=jnp.float32) * s(D)
        W_v = jax.random.normal(ks[6], (D, D), dtype=jnp.float32) * s(D)
        W_out = jax.random.normal(ks[7], (INNER, DIM), dtype=jnp.float32) * s(INNER)
        b_out = jnp.zeros((DIM,), dtype=jnp.float32)
        temperature = jnp.ones((1, H, 1, 1), dtype=jnp.float32) * 0.5
        return {'x': x, 'W_fx': W_fx, 'b_fx': b_fx, 'W_x': W_x, 'b_x': b_x, 'W_slice': W_slice, 'b_slice': b_slice, 'W_q': W_q, 'W_k': W_k, 'W_v': W_v, 'W_out': W_out, 'b_out': b_out, 'temperature': temperature}
    _L3_ffn_all = _L3_ffn_setup()
    _L3_ffn_in = {k: v for k, v in _L3_ffn_all.items() if k in ('W_fx', 'b_fx', 'W_x', 'b_x', 'W_slice', 'b_slice', 'W_q', 'W_k', 'W_v', 'W_out', 'b_out', 'temperature')}
    del _L3_ffn_all
    return {'x': x, 'src': src, 'dst': dst, 'edge_attr_64': edge_attr_64, 'L0_gnn_W_fc': _L0_gnn_in['W_fc'], 'L0_gnn_W_e': _L0_gnn_in['W_e'], 'L0_gnn_attn_h': _L0_gnn_in['attn_h'], 'L0_gnn_attn_e': _L0_gnn_in['attn_e'], 'L0_gnn_attn_t': _L0_gnn_in['attn_t'], 'L0_gnn_bias': _L0_gnn_in['bias'], 'L0_ffn_Wr': _L0_ffn_in['Wr'], 'L0_ffn_br': _L0_ffn_in['br'], 'L0_ffn_W1': _L0_ffn_in['W1'], 'L0_ffn_b1': _L0_ffn_in['b1'], 'L0_ffn_g1': _L0_ffn_in['g1'], 'L0_ffn_be1': _L0_ffn_in['be1'], 'L0_ffn_m1': _L0_ffn_in['m1'], 'L0_ffn_v1': _L0_ffn_in['v1'], 'L0_ffn_W2': _L0_ffn_in['W2'], 'L0_ffn_b2': _L0_ffn_in['b2'], 'L0_ffn_g2': _L0_ffn_in['g2'], 'L0_ffn_be2': _L0_ffn_in['be2'], 'L0_ffn_m2': _L0_ffn_in['m2'], 'L0_ffn_v2': _L0_ffn_in['v2'], 'L0_ffn_Wo': _L0_ffn_in['Wo'], 'L0_ffn_bo': _L0_ffn_in['bo'], 'L1_gnn_Wq': _L1_gnn_in['Wq'], 'L1_gnn_bq': _L1_gnn_in['bq'], 'L1_gnn_Wk': _L1_gnn_in['Wk'], 'L1_gnn_bk': _L1_gnn_in['bk'], 'L1_gnn_Wv': _L1_gnn_in['Wv'], 'L1_gnn_bv': _L1_gnn_in['bv'], 'L1_gnn_Ws': _L1_gnn_in['Ws'], 'L1_gnn_bs': _L1_gnn_in['bs'], 'L1_gnn_Wl': _L1_gnn_in['Wl'], 'L1_gnn_bl': _L1_gnn_in['bl'], 'L1_gnn_Wr': _L1_gnn_in['Wr'], 'L1_gnn_gamma': _L1_gnn_in['gamma'], 'L1_gnn_beta': _L1_gnn_in['beta'], 'L1_gnn_alpha_res': _L1_gnn_in['alpha_res'], 'L1_ffn_Wg': _L1_ffn_in['Wg'], 'L1_ffn_bg': _L1_ffn_in['bg'], 'L1_ffn_bias': _L1_ffn_in['bias'], 'L1_ffn_W1': _L1_ffn_in['W1'], 'L1_ffn_b1': _L1_ffn_in['b1'], 'L1_ffn_W2': _L1_ffn_in['W2'], 'L1_ffn_b2': _L1_ffn_in['b2'], 'L2_gnn_W': _L2_gnn_in['W'], 'L2_gnn_att_src': _L2_gnn_in['att_src'], 'L2_gnn_att_dst': _L2_gnn_in['att_dst'], 'L2_gnn_bias': _L2_gnn_in['bias'], 'L2_ffn_router_w': _L2_ffn_in['router_w'], 'L2_ffn_w1': _L2_ffn_in['w1'], 'L2_ffn_b1': _L2_ffn_in['b1'], 'L2_ffn_w2': _L2_ffn_in['w2'], 'L2_ffn_b2': _L2_ffn_in['b2'], 'L3_gnn_W_in': _L3_gnn_in['W_in'], 'L3_gnn_b_in': _L3_gnn_in['b_in'], 'L3_gnn_W_u0': _L3_gnn_in['W_u0'], 'L3_gnn_b_u0': _L3_gnn_in['b_u0'], 'L3_gnn_W_u1': _L3_gnn_in['W_u1'], 'L3_gnn_b_u1': _L3_gnn_in['b_u1'], 'L3_gnn_W_ro': _L3_gnn_in['W_ro'], 'L3_gnn_b_ro': _L3_gnn_in['b_ro'], 'L3_ffn_W_fx': _L3_ffn_in['W_fx'], 'L3_ffn_b_fx': _L3_ffn_in['b_fx'], 'L3_ffn_W_x': _L3_ffn_in['W_x'], 'L3_ffn_b_x': _L3_ffn_in['b_x'], 'L3_ffn_W_slice': _L3_ffn_in['W_slice'], 'L3_ffn_b_slice': _L3_ffn_in['b_slice'], 'L3_ffn_W_q': _L3_ffn_in['W_q'], 'L3_ffn_W_k': _L3_ffn_in['W_k'], 'L3_ffn_W_v': _L3_ffn_in['W_v'], 'L3_ffn_W_out': _L3_ffn_in['W_out'], 'L3_ffn_b_out': _L3_ffn_in['b_out'], 'L3_ffn_temperature': _L3_ffn_in['temperature']}

def reference(x, src, dst, edge_attr_64, L0_gnn_W_fc, L0_gnn_W_e, L0_gnn_attn_h, L0_gnn_attn_e, L0_gnn_attn_t, L0_gnn_bias, L0_ffn_Wr, L0_ffn_br, L0_ffn_W1, L0_ffn_b1, L0_ffn_g1, L0_ffn_be1, L0_ffn_m1, L0_ffn_v1, L0_ffn_W2, L0_ffn_b2, L0_ffn_g2, L0_ffn_be2, L0_ffn_m2, L0_ffn_v2, L0_ffn_Wo, L0_ffn_bo, L1_gnn_Wq, L1_gnn_bq, L1_gnn_Wk, L1_gnn_bk, L1_gnn_Wv, L1_gnn_bv, L1_gnn_Ws, L1_gnn_bs, L1_gnn_Wl, L1_gnn_bl, L1_gnn_Wr, L1_gnn_gamma, L1_gnn_beta, L1_gnn_alpha_res, L1_ffn_Wg, L1_ffn_bg, L1_ffn_bias, L1_ffn_W1, L1_ffn_b1, L1_ffn_W2, L1_ffn_b2, L2_gnn_W, L2_gnn_att_src, L2_gnn_att_dst, L2_gnn_bias, L2_ffn_router_w, L2_ffn_w1, L2_ffn_b1, L2_ffn_w2, L2_ffn_b2, L3_gnn_W_in, L3_gnn_b_in, L3_gnn_W_u0, L3_gnn_b_u0, L3_gnn_W_u1, L3_gnn_b_u1, L3_gnn_W_ro, L3_gnn_b_ro, L3_ffn_W_fx, L3_ffn_b_fx, L3_ffn_W_x, L3_ffn_b_x, L3_ffn_W_slice, L3_ffn_b_slice, L3_ffn_W_q, L3_ffn_W_k, L3_ffn_W_v, L3_ffn_W_out, L3_ffn_b_out, L3_ffn_temperature):
    import jax
    import jax.numpy as jnp

    def _L0_gnn_ref(feat, edge_attr, src, dst, W_fc, W_e, attn_h, attn_e, attn_t, bias):
        import jax, jax.numpy as jnp
        import numpy as np
        N_NODES = 50000
        N_EDGES = 25000
        IN_DIM = 256
        E_DIM = 64
        N_HEADS = 8
        OUT_DIM = 32
        NEG_SLOPE = 0.2
        N = feat.shape[0]
        H, D = attn_h.shape
        ft = (feat @ W_fc).reshape(N, H, D)
        eh = jnp.einsum('nhd,hd->nh', ft, attn_h)
        et = jnp.einsum('nhd,hd->nh', ft, attn_t)
        fe = (edge_attr @ W_e).reshape(-1, H, D)
        ee = jnp.einsum('ehd,hd->eh', fe, attn_e)
        e = jax.nn.leaky_relu(eh[src] + ee + et[dst], negative_slope=NEG_SLOPE)
        e_max = jax.ops.segment_max(e, dst, num_segments=N)
        e_max = jax.lax.stop_gradient(jnp.where(jnp.isfinite(e_max), e_max, 0.0))
        ex = jnp.exp(e - e_max[dst])
        denom = jax.ops.segment_sum(ex, dst, num_segments=N)
        a = ex / denom[dst]
        msg = ft[src] * a[:, :, None]
        rst = jax.ops.segment_sum(msg, dst, num_segments=N)
        rst = rst + bias[None, :, :]
        return rst.reshape(N, H * D)

    def _L0_ffn_ref(x, Wr, br, W1, b1, g1, be1, m1, v1, W2, b2, g2, be2, m2, v2, Wo, bo):
        import jax, jax.numpy as jnp
        import numpy as np
        BN_EPS = 0.001

        def _bn(h, g, b, m, v):
            return g * (h - m) * jax.lax.rsqrt(v + BN_EPS) + b
        feat = jnp.mean(x, axis=0)
        w = jax.nn.softmax(feat @ Wr + br, axis=-1)
        h = jnp.einsum('bfd,edh->bfeh', x, W1) + b1
        h = jax.nn.relu(_bn(h, g1, be1, m1, v1))
        h = jnp.einsum('bfeh,ehk->bfek', h, W2) + b2
        h = jax.nn.relu(_bn(h, g2, be2, m2, v2))
        y = jnp.einsum('bfeh,ehd->bfed', h, Wo) + bo
        return jnp.einsum('bfed,fe->bfd', y, w)

    def _L1_gnn_ref(x, edge_index, Wq, bq, Wk, bk, Wv, bv, Ws, bs, Wl, bl, Wr, gamma, beta, alpha_res):
        import jax, jax.numpy as jnp
        import numpy as np
        N_NODES = 10000
        N_EDGES = 10000
        D = 256
        L = 3
        BN_EPS = 1e-05

        def _segment_softmax(logits, seg, num_segments):
            m = jax.ops.segment_max(logits, seg, num_segments=num_segments)
            e = jnp.exp(logits - m[seg])
            s = jax.ops.segment_sum(e, seg, num_segments=num_segments)
            return e / s[seg]
        src, dst = (edge_index[0], edge_index[1])
        n, d = x.shape
        q = x @ Wq + bq
        k = x @ Wk + bk
        v = x @ Wv + bv
        logits = jnp.sum(q[dst] * k[src], axis=-1) / jnp.sqrt(jnp.asarray(d, x.dtype))
        attn = _segment_softmax(logits, dst, n)
        agg = jax.ops.segment_sum(attn[:, None] * v[src], dst, num_segments=n)
        h = agg + x @ Ws + bs
        h = jax.nn.relu(h)
        deg = jax.ops.segment_sum(jnp.ones((src.shape[0],), x.dtype), dst, num_segments=n)
        deg = jnp.maximum(deg, 1.0)[:, None]
        prev = h
        bn_scale = 1.0 / jnp.sqrt(1.0 + BN_EPS)
        al = jax.nn.sigmoid(alpha_res)
        for i in range(Wl.shape[0]):
            mean_nb = jax.ops.segment_sum(h[src], dst, num_segments=n) / deg
            z = mean_nb @ Wl[i] + bl[i] + h @ Wr[i]
            z = z * bn_scale * gamma[i] + beta[i]
            z = al * z + (1.0 - al) * prev
            h = jax.nn.relu(z)
            prev = h
        return h

    def _L1_ffn_ref(x, Wg, bg, bias, W1, b1, W2, b2):
        import jax, jax.numpy as jnp
        import numpy as np
        D_MODEL = 256
        EXPERT_DIM = 512
        NUM_EXPERTS = 8
        TOP_K = 2
        SEQ_LEN = 64
        BATCH = 2
        x_flat = x.reshape(-1, D_MODEL)
        gate_logits = x_flat @ Wg + bg + bias
        topk_vals, topk_idx = jax.lax.top_k(gate_logits, TOP_K)
        topk_w = jax.nn.softmax(topk_vals, axis=-1)
        combine = (jax.nn.one_hot(topk_idx, NUM_EXPERTS, dtype=x.dtype) * topk_w[..., None]).sum(axis=1)
        h = jax.nn.relu(jnp.einsum('td,edh->teh', x_flat, W1) + b1)
        y = jnp.einsum('teh,ehd->ted', h, W2) + b2
        out = jnp.einsum('ted,te->td', y, combine)
        return out.reshape(x.shape)

    def _L2_gnn_ref(x, edge_index, W, att_src, att_dst, bias):
        import jax, jax.numpy as jnp
        import numpy as np
        N_NODES = 50000
        N_EDGES = 25000
        IN_DIM = 256
        HEADS = 4
        HEAD_DIM = 64
        NEG_SLOPE = 0.2
        N = x.shape[0]
        loops = jnp.arange(N, dtype=edge_index.dtype)
        src = jnp.concatenate([edge_index[0], loops])
        dst = jnp.concatenate([edge_index[1], loops])
        h = (x @ W).reshape(N, HEADS, HEAD_DIM)
        a_src = jnp.einsum('nhd,hd->nh', h, att_src)
        a_dst = jnp.einsum('nhd,hd->nh', h, att_dst)
        e = a_src[src] + a_dst[dst]
        e = jax.nn.leaky_relu(e, NEG_SLOPE)
        m = jax.ops.segment_max(e, dst, num_segments=N)
        e = jnp.exp(e - m[dst])
        denom = jax.ops.segment_sum(e, dst, num_segments=N)
        alpha = e / denom[dst]
        msg = alpha[:, :, None] * h[src]
        out = jax.ops.segment_sum(msg, dst, num_segments=N)
        return out.reshape(N, HEADS * HEAD_DIM) + bias

    def _L2_ffn_ref(input_embeddings, router_w, w1, b1, w2, b2):
        import jax, jax.numpy as jnp
        import numpy as np
        NUM_EXPERTS = 8
        TOP_K = 2
        B, S, D = (8, 256, 256)

        def _moe(tokens, router_w, w1, b1, w2, b2):
            N = tokens.shape[0]
            E = router_w.shape[0]
            logits = tokens.astype(jnp.float32) @ router_w.astype(jnp.float32).T
            probs = jax.nn.softmax(logits, axis=-1)
            rw, re = jax.lax.top_k(probs, TOP_K)
            if TOP_K > 1:
                rw = rw / jnp.maximum(rw.sum(-1, keepdims=True), 1e-12)
            rw = rw.astype(tokens.dtype)
            combine = jnp.zeros((N, E), tokens.dtype).at[jnp.arange(N)[:, None], re].set(rw)
            out = tokens
            for e in range(E):
                h = jax.nn.gelu(tokens @ w1[e] + b1[e], approximate=False)
                y = h @ w2[e] + b2[e]
                out = out + combine[:, e:e + 1] * y
            return out
        b, s, d = input_embeddings.shape
        tokens = input_embeddings.reshape(b * s, d)
        return _moe(tokens, router_w, w1, b1, w2, b2).reshape(b, s, d)

    def _L3_gnn_ref(x, he, src, dst, W_in, b_in, W_u0, b_u0, W_u1, b_u1, W_ro, b_ro):
        import jax, jax.numpy as jnp
        import numpy as np
        N_NODES = 50000
        N_EDGES = 25000
        FEAT = 256
        EDIM = 64
        OUT = 256
        n = x.shape[0]
        hv = x @ W_in + b_in
        deg = jax.ops.segment_sum(jnp.ones_like(dst, jnp.float32), dst, num_segments=n)
        has_in = (deg > 0)[:, None]
        for W, b in ((W_u0, b_u0), (W_u1, b_u1)):
            m = jnp.concatenate([hv[src], he], axis=-1)
            m = jax.nn.relu(m @ W + b)
            msg = jax.ops.segment_max(m, dst, num_segments=n)
            hv = jnp.where(has_in, msg + hv, hv)
        return jax.nn.relu(hv @ W_ro + b_ro)

    def _L3_ffn_ref(x, W_fx, b_fx, W_x, b_x, W_slice, b_slice, W_q, W_k, W_v, W_out, b_out, temperature):
        import jax, jax.numpy as jnp
        import numpy as np
        DIM = 256
        H = 8
        D = 64
        G = 64
        INNER = H * D
        SCALE = D ** (-0.5)
        B, N, _ = x.shape
        fx_mid = (x @ W_fx + b_fx).reshape(B, N, H, D).transpose(0, 2, 1, 3)
        x_mid = (x @ W_x + b_x).reshape(B, N, H, D).transpose(0, 2, 1, 3)
        temp = jnp.clip(temperature, 0.1, 5.0)
        slice_weights = jax.nn.softmax((x_mid @ W_slice + b_slice) / temp, axis=-1)
        slice_norm = slice_weights.sum(axis=2)
        slice_token = jnp.einsum('bhnc,bhng->bhgc', fx_mid, slice_weights)
        slice_token = slice_token / (slice_norm[..., None] + 1e-05)
        q = slice_token @ W_q
        k = slice_token @ W_k
        v = slice_token @ W_v
        attn = jax.nn.softmax(jnp.einsum('bhgc,bhkc->bhgk', q, k) * SCALE, axis=-1)
        out_slice = jnp.einsum('bhgk,bhkc->bhgc', attn, v)
        out_x = jnp.einsum('bhgc,bhng->bhnc', out_slice, slice_weights)
        out_x = out_x.transpose(0, 2, 1, 3).reshape(B, N, INNER)
        return out_x @ W_out + b_out
    edge_index = jnp.stack([src, dst])
    x = x + _L0_gnn_ref(_layernorm(x, axis=-1), edge_attr_64, src, dst, L0_gnn_W_fc, L0_gnn_W_e, L0_gnn_attn_h, L0_gnn_attn_e, L0_gnn_attn_t, L0_gnn_bias)
    x = x + _L0_ffn_ref(_layernorm(x, axis=-1)[None], L0_ffn_Wr, L0_ffn_br, L0_ffn_W1, L0_ffn_b1, L0_ffn_g1, L0_ffn_be1, L0_ffn_m1, L0_ffn_v1, L0_ffn_W2, L0_ffn_b2, L0_ffn_g2, L0_ffn_be2, L0_ffn_m2, L0_ffn_v2, L0_ffn_Wo, L0_ffn_bo)[0]
    x = x + _L1_gnn_ref(_layernorm(x, axis=-1), edge_index, L1_gnn_Wq, L1_gnn_bq, L1_gnn_Wk, L1_gnn_bk, L1_gnn_Wv, L1_gnn_bv, L1_gnn_Ws, L1_gnn_bs, L1_gnn_Wl, L1_gnn_bl, L1_gnn_Wr, L1_gnn_gamma, L1_gnn_beta, L1_gnn_alpha_res)
    x = x + _L1_ffn_ref(_layernorm(x, axis=-1)[None], L1_ffn_Wg, L1_ffn_bg, L1_ffn_bias, L1_ffn_W1, L1_ffn_b1, L1_ffn_W2, L1_ffn_b2)[0]
    x = x + _L2_gnn_ref(_layernorm(x, axis=-1), edge_index, L2_gnn_W, L2_gnn_att_src, L2_gnn_att_dst, L2_gnn_bias)
    x = x + _L2_ffn_ref(_layernorm(x, axis=-1)[None], L2_ffn_router_w, L2_ffn_w1, L2_ffn_b1, L2_ffn_w2, L2_ffn_b2)[0]
    x = x + _L3_gnn_ref(_layernorm(x, axis=-1), edge_attr_64, src, dst, L3_gnn_W_in, L3_gnn_b_in, L3_gnn_W_u0, L3_gnn_b_u0, L3_gnn_W_u1, L3_gnn_b_u1, L3_gnn_W_ro, L3_gnn_b_ro)
    x = x + _L3_ffn_ref(_layernorm(x, axis=-1)[None], L3_ffn_W_fx, L3_ffn_b_fx, L3_ffn_W_x, L3_ffn_b_x, L3_ffn_W_slice, L3_ffn_b_slice, L3_ffn_W_q, L3_ffn_W_k, L3_ffn_W_v, L3_ffn_W_out, L3_ffn_b_out, L3_ffn_temperature)[0]
    return x

_drawn_inputs = setup_inputs


def setup_inputs(seed=0):
    import zlib

    import numpy as np

    out = dict(_drawn_inputs(seed))
    spreads = {'L0_gnn_bias': (0.0, 0.1),
     'L0_ffn_br': (0.0, 0.1),
     'L0_ffn_b1': (0.0, 0.3),
     'L0_ffn_g1': (1.0, 0.2),
     'L0_ffn_be1': (0.0, 0.304),
     'L0_ffn_m1': (0.0, 0.308),
     'L0_ffn_v1': (1.0, 0.588),
     'L0_ffn_b2': (0.0, 0.1),
     'L0_ffn_g2': (1.0, 0.2),
     'L0_ffn_be2': (0.0, 0.1),
     'L0_ffn_m2': (0.0, 0.1),
     'L0_ffn_v2': (1.0, 0.538),
     'L0_ffn_bo': (0.0, 0.1),
     'L1_gnn_bq': (0.0, 0.8),
     'L1_gnn_bk': (0.0, 0.8),
     'L1_gnn_bv': (0.0, 0.33),
     'L1_gnn_bs': (0.0, 0.33),
     'L1_gnn_bl': (0.0, 0.1),
     'L1_ffn_bias': (0.0, 0.28),
     'L2_gnn_bias': (0.0, 0.1),
     'L2_ffn_b1': (0.0, 0.531),
     'L2_ffn_b2': (0.0, 0.35),
     'L3_gnn_b_in': (0.0, 0.1),
     'L3_gnn_b_u0': (0.0, 0.354),
     'L3_gnn_b_u1': (0.0, 0.441),
     'L3_gnn_b_ro': (0.0, 0.438),
     'L3_ffn_b_fx': (0.0, 0.318),
     'L3_ffn_b_x': (0.0, 0.8),
     'L3_ffn_b_slice': (0.0, 0.8),
     'L3_ffn_b_out': (0.0, 0.335),
     'L3_ffn_temperature': (0.5, 0.6)}
    factors = {'L1_ffn_bg': 4.802,
     'L1_ffn_b1': 8.0,
     'L1_ffn_b2': 3.664,
     'L3_ffn_W_x': 8.0,
     'L3_ffn_W_slice': 8.0,
     'L3_ffn_W_q': 8.0,
     'L3_ffn_W_k': 8.0}
    for name, (base, spread) in spreads.items():
        noise = np.random.default_rng([zlib.crc32(name.encode()), seed]).standard_normal(out[name].shape)
        drawn = base * np.exp(spread * noise) if base else spread * noise
        out[name] = jnp.asarray(drawn.astype(out[name].dtype))
    for name, factor in factors.items():
        out[name] = (out[name] * factor).astype(out[name].dtype)
    return out
```

```python
from contextlib import ExitStack

import numpy as np
import concourse.bass as bass
from concourse import mybir

ALU = mybir.AluOpType
ACT = mybir.ActivationFunctionType
F32 = mybir.dt.float32
BF16 = mybir.dt.bfloat16
I32 = mybir.dt.int32
U32 = mybir.dt.uint32
AX_X = mybir.AxisListType.X
ds = bass.ds

P = 128
N = 3125
NT = -(-N // P)
NP_ = NT * P
E = 50000
D = 256
KD = D // P
EA = 64
STEPS = 416
GROUPS = 4
SPG = STEPS // GROUPS
SLOTS = STEPS * P
ROWS = -(-E // P) + 1
EP = ROWS * P
ER, EC = 125, E // 125
BIG = 1.0e30
U = 8
HALF = 4
NE = 8
CH = 5
TOK = CH * P
assert STEPS >= ROWS - 1 + NT - 1 and STEPS % U == 0 and NT % CH == 0
AC = 272


class Order:

    def __init__(self, eng, sem, start=0):
        self.eng, self.sem, self.at = eng, sem, start

    def then(self, ins):
        ins.then_inc(self.sem, 1)
        self.at = self.at + 1
        return ins

    def wait(self):
        self.eng.wait_ge(self.sem, self.at)

    def link(self, ins):
        self.then(ins)
        self.wait()


class Phase:

    def __init__(self, nc):
        self.nc, self.ctx, self.sems = nc, ExitStack(), []

    def __enter__(self):
        return self

    def sem(self, name):
        s = self.nc.alloc_semaphore(name + "_" + str(self.nc.next_id()))
        self.sems.append(s)
        return s

    def sb(self, name, shape, dt):
        return self.ctx.enter_context(self.nc.sbuf_tensor(name + "_" + str(self.nc.next_id()), shape, dt))

    def ps(self, name, shape, dt=F32):
        return self.ctx.enter_context(self.nc.psum_tensor(name + "_" + str(self.nc.next_id()), shape, dt))

    def __exit__(self, *a):
        self.ctx.close()
        if a[0] is None:
            self.nc.clear_and_free_semaphores(self.sems)
            self.nc.all_engine_barrier()


class Net:
    pass


def edge_steps(nc, g):
    with Phase(nc) as ph:
        sb, ps, sem = ph.sb, ph.ps, ph.sem
        dst_i = sb("dst_i", [ER, EC], I32)
        dst_f = sb("dst_f", [ER, EC], F32)
        below = sb("below", [ER, EC], F32)
        cnt = sb("cnt", [ER, NT + 1], F32)
        ones = sb("ones", [P, P], F32)
        pt = sb("pt", [P, NT + 1], F32)
        inside = sb("inside", [P, NT], F32)
        ends_i = sb("ends_i", [P, 2, NT], I32)
        rows_i = sb("rows_i", [P, 2, NT], I32)
        rows = sb("rows", [P, 2, NT], F32)
        span = sb("span", [P, NT], F32)
        nst = sb("nst", [P, NT], F32)
        cum = sb("cum", [P, NT], F32)
        first = sb("first", [P, NT], F32)
        base = sb("base", [P, NT + 1], F32)
        dbase = sb("dbase", [P, NT], F32)
        kcol = sb("kcol", [SPG, GROUPS], F32)
        begun = sb("begun", [SPG, NT], F32)
        junk = sb("junk", [SPG, NT], F32)
        off = sb("off", [SPG, GROUPS], F32)
        row_f = sb("row_f", [SPG, GROUPS], F32)
        tile1 = sb("tile1", [SPG, GROUPS], F32)
        tile0 = sb("tile0", [SPG, GROUPS], F32)
        tile_i = sb("tile_i", [SPG, GROUPS], I32)
        cnt_ps = ps("cnt_ps", [P, NT + 1])
        loaded, consts, counted, summed, done, own, stored, gown = (
            sem(x) for x in ("loaded", "consts", "counted", "summed", "done", "own", "stored", "gown"))
        with nc.Block() as block:
            @block.sync
            def _(sp):
                sp.dma_start(dst_i[:], g.ins["dst_grid"]).then_inc(loaded, 16)
                sp.wait_ge(done, 1)
                with nc.allow_non_contiguous_dma("step tables of 4-byte elements"):
                    sp.dma_start(g.row_dram.rearrange("(g p) -> p g", g=GROUPS), g.row_b[:]).then_inc(stored, 16)
                    sp.dma_start(g.tile_dram.rearrange("(g p) -> p g", g=GROUPS), tile_i[:]).then_inc(stored, 16)
                sp.wait_ge(stored, 32)
                sp.dma_start(g.row_row[:], g.row_dram.rearrange("(a n) -> a n", a=1)).then_inc(stored, 16)
                sp.dma_start(g.tile_row[:], g.tile_dram.rearrange("(a n) -> a n", a=1)).then_inc(stored, 16)
                sp.wait_ge(stored, 64)

            @block.gpsimd
            def _(pool):
                o = Order(pool, gown)
                o.then(nc.gpsimd.memset(ones[:], 1.0))
                o.then(nc.gpsimd.memset(g.ident[:], 0.0))
                o.then(nc.gpsimd.memset(g.identb[:], 0.0))
                o.then(nc.gpsimd.iota(kcol[:], [[SPG, GROUPS]], 0, 1, allow_small_or_imprecise_dtypes=True))
                o.then(nc.gpsimd.iota(g.pidx[:], [[1, 1]], 0, 1, allow_small_or_imprecise_dtypes=True))
                o.then(nc.gpsimd.iota(g.lane[:], [[1, P]], 0, 0, allow_small_or_imprecise_dtypes=True))
                o.wait()
                for m in (g.ident, g.identb):
                    nc.gpsimd.affine_select(out=m[:], in_=m[:], compare_op=ALU.not_equal, fill=1.0, base=0,
                                            pattern=[[-1, P]], channel_multiplier=1).then_inc(consts, 1)

            @block.vector
            def _(dve):
                o = Order(dve, own)
                v = nc.vector
                dve.wait_ge(loaded, 16)
                dve.wait_ge(consts, 2)
                o.link(v.tensor_copy(dst_f[:], dst_i[:]))
                for n in range(NT + 1):
                    o.link(v.tensor_scalar(below[:], dst_f[:], float(P * n), 0.0, ALU.is_lt, ALU.add,
                                           accum_out=cnt[:, n:n + 1]))
                v.memset(base[:], 0.0).then_inc(counted, 1)
                dve.wait_ge(counted, 1)
                dve.wait_ge(summed, 1)
                o.link(v.tensor_copy(pt[:], cnt_ps[:]))
                o.link(v.tensor_sub(inside[:], pt[:, 1:NT + 1], pt[:, 0:NT]))
                o.then(v.tensor_copy(ends_i[:, 0, :], pt[:, 0:NT]))
                o.link(v.tensor_scalar(ends_i[:, 1, :], pt[:, 1:NT + 1], -1.0, None, ALU.add))
                o.link(v.tensor_scalar(rows_i[:], ends_i[:], 7, None, ALU.arith_shift_right))
                o.link(v.tensor_copy(rows[:], rows_i[:]))
                o.link(v.scalar_tensor_tensor(span[:], rows[:, 1, :], 1.0, rows[:, 0, :], ALU.add, ALU.subtract))
                o.link(v.scalar_tensor_tensor(nst[:], inside[:], 0.0, span[:], ALU.is_gt, ALU.mult))
                o.link(v.tensor_tensor_scan(cum[:], ones[:, 0:NT], nst[:], 0.0, ALU.mult, ALU.add))
                o.link(v.tensor_sub(first[:], cum[:], nst[:]))
                o.link(v.tensor_sub(base[:, 1:NT + 1], rows[:, 0, :], first[:]))
                o.link(v.tensor_sub(dbase[:], base[:, 1:NT + 1], base[:, 0:NT]))
                for q in range(GROUPS):
                    o.link(v.tensor_scalar(begun[:], first[0:SPG, :], kcol[:, q:q + 1], None, ALU.is_le))
                    o.link(v.tensor_tensor_reduce(junk[:], begun[:], dbase[0:SPG, :], 1.0, 0.0, ALU.mult, ALU.add,
                                                  off[:, q:q + 1]))
                    o.link(v.reduce_sum(tile1[:, q:q + 1], begun[:], AX_X))
                o.link(v.tensor_add(row_f[:], kcol[:], off[:]))
                o.link(v.tensor_scalar(g.row_b[:], row_f[:], float(ROWS - 1), None, ALU.min))
                o.link(v.tensor_scalar(tile0[:], tile1[:], -1.0, None, ALU.add))
                o.link(v.tensor_copy(tile_i[:], tile0[:]))
                v.tensor_scalar(g.node0_b[:], tile0[:], float(P), None, ALU.mult).then_inc(done, 1)

            @block.tensor
            def _(pe):
                pe.wait_ge(counted, 1)
                nc.tensor.matmul(cnt_ps[:], ones[0:ER, :], cnt[:], start=True, stop=True).then_inc(summed, 1)


def slot_tables(nc, g):
    with Phase(nc) as ph:
        sb, ps, sem = ph.sb, ph.ps, ph.sem
        ids_i = sb("ids_i", [SPG, GROUPS, 3, P], I32)
        ids_f = sb("ids_f", [SPG, GROUPS, 3, P], F32)
        loc = sb("loc", [SPG, GROUPS, P], F32)
        ok = sb("ok", [SPG, GROUPS, P], F32)
        tmp = sb("tmp", [SPG, GROUPS, P], F32)
        tabs = sb("tabs", [SPG, 4, GROUPS, P], F32)
        prev = sb("prev", [SPG, GROUPS, P], F32)
        same = sb("same", [SPG, GROUPS, P], BF16)
        loc_h = sb("loc_h", [SPG, GROUPS, P], BF16)
        front = sb("front", [1, 1], F32)
        turned = ps("turned", [P, 2, 512])
        loaded, own, tabbed, turn, taken, sent, sames, fr, loc_out = (sem(x) for x in (
            "loaded", "own", "tabbed", "turn", "taken", "sent", "sames", "fr", "loc_out"))
        outs = [g.src_a, g.dst_a, g.loc_a, g.last_a]
        with nc.Block() as block:
            @block.gpsimd
            def _(pool):
                for q in range(GROUPS):
                    nc.gpsimd.indirect_dma_start(
                        out=ids_i[:, q, :, :].rearrange("p c l -> p (c l)"), out_offset=None, in_=g.ins["ids"],
                        in_offset=bass.IndirectOffsetOnAxis(ap=g.row_b[:, q:q + 1], axis=0)).then_inc(loaded, 16)

            @block.sync
            def _(sp):
                sp.wait_ge(tabbed, 2)
                sp.wait_ge(fr, 1)
                sp.dma_start(g.loc_slots.rearrange("(g p l) -> p g l", g=GROUPS, l=P), loc_h[:]).then_inc(loc_out, 16)
                sp.dma_start(g.dst_slots[1:SLOTS + 1].rearrange("(g p l) -> p g l", g=GROUPS, l=P),
                             tabs[:, 1, :, :]).then_inc(sent, 16)
                sp.dma_start(g.dst_slots[0:1].rearrange("(a n) -> a n", a=1), front[:]).then_inc(sent, 16)
                sp.wait_ge(sent, 32)
                sp.dma_start(prev[:], g.dst_slots[0:SLOTS].rearrange("(g p l) -> p g l", g=GROUPS, l=P)).then_inc(sent, 16)
                sp.wait_ge(sames, 1)
                sp.dma_start(g.same_slots.rearrange("(g p l) -> p g l", g=GROUPS, l=P), same[:]).then_inc(sent, 16)
                sp.wait_ge(sent, 64)
                sp.wait_ge(loc_out, 16)

            @block.vector
            def _(dve):
                o = Order(dve, own)
                v = nc.vector
                v.memset(front[:], -2.0).then_inc(fr, 1)
                dve.wait_ge(loaded, 16 * GROUPS)
                o.link(v.tensor_copy(ids_f[:], ids_i[:]))
                src, dst, nxt = (ids_f[:, :, c, :] for c in range(3))
                for q in range(GROUPS):
                    o.then(v.tensor_scalar(loc[:, q, :], dst[:, q, :], g.node0_b[:, q:q + 1], None, ALU.subtract))
                o.wait()
                o.then(v.tensor_copy(tabs[:, 0, :, :], src))
                o.link(v.tensor_scalar(tmp[:], loc[:], 0.0, None, ALU.is_ge))
                o.link(v.scalar_tensor_tensor(ok[:], loc[:], float(P), tmp[:], ALU.is_lt, ALU.mult))
                o.link(v.scalar_tensor_tensor(tmp[:], dst, 1.0, ok[:], ALU.add, ALU.mult))
                o.link(v.tensor_scalar(tabs[:, 1, :, :], tmp[:], -1.0, None, ALU.add))
                o.link(v.scalar_tensor_tensor(tmp[:], loc[:], 1.0, ok[:], ALU.add, ALU.mult))
                o.link(v.tensor_scalar(tabs[:, 2, :, :], tmp[:], -1.0, None, ALU.add))
                o.link(v.tensor_tensor(ok[:], dst, nxt, ALU.not_equal))
                o.link(v.tensor_mul(tmp[:], tmp[:], ok[:]))
                v.tensor_scalar(tabs[:, 3, :, :], tmp[:], -1.0, None, ALU.add).then_inc(tabbed, 1)
                v.tensor_copy(loc_h[:], tabs[:, 2, :, :]).then_inc(tabbed, 1)
                n = 0
                for q in range(GROUPS):
                    for b in range(2):
                        dve.wait_ge(turn, n + 1)
                        for c in range(2):
                            last = v.tensor_copy(outs[2 * b + c][:, q * SPG:(q + 1) * SPG], turned[:, n % 2, c * P:c * P + SPG])
                        last.then_inc(taken, 1)
                        n += 1
                dve.wait_ge(sent, 48)
                v.tensor_tensor(same[:], prev[:], tabs[:, 1, :, :], ALU.is_equal).then_inc(sames, 1)

            @block.tensor
            def _(pe):
                pe.wait_ge(tabbed, 1)
                n = 0
                for q in range(GROUPS):
                    for b in range(2):
                        if n >= 2:
                            pe.wait_ge(taken, n - 1)
                        for c in range(2):
                            last = nc.tensor.transpose(turned[:, n % 2, c * P:c * P + SPG], tabs[:, 2 * b + c, q, :],
                                                       g.ident[0:SPG, 0:SPG])
                        last.then_inc(turn, 1)
                        n += 1


def by_partition(ap):
    return ap.rearrange("(k p) c -> p k c", p=P)


def tile_rows(ap):
    return ap.rearrange("(t p) c -> p t c", p=P)


def load_all(nc, ph, eng, pairs, name):
    s = ph.sem(name)
    for out, in_ in pairs:
        eng.dma_start(out, in_).then_inc(s, 16)
    return s, 16 * len(pairs)


def node_rows(nc, g, srcs, w_drams, cols, bias, sinks, ln=False, xn=None, xt=None, relu_add=None):
    S = len(srcs)
    NB = max(1, -(-cols // 512))
    DEPTH = 4 // NB
    with Phase(nc) as ph:
        sb, ps, sem = ph.sb, ph.ps, ph.sem
        w = sb("w", [P, S, KD, max(cols, 8)], F32)
        brow = sb("brow", [1, max(cols, 8)], F32)
        one = sb("one", [1, P], F32)
        rows = sb("rows", [P, CH, S, D], F32)
        rows_t = sb("rows_t", [P, CH, S * KD, P], F32)
        stats = sb("stats", [P, CH, 6], F32)
        mv = sb("mv", [P, CH, 2], F32)
        veps = sb("veps", [P, CH], F32)
        std = sb("std", [P, CH], F32)
        rstd = sb("rstd", [P, CH], F32)
        ps_t = ps("ps_t", [P, 2, 512])
        ps_o = ps("ps_o", [P, 4, 512])
        w_in, own, one_set, rows_set, var_set, std_set, turned, taken, multiplied, evacuated, stored, passed = (sem(x) for x in (
            "w_in", "own", "one_set", "rows_set", "var_set", "std_set", "turned", "taken", "multiplied", "evacuated", "stored", "passed"))
        WL = 16 * (len(w_drams) + (1 if bias is not None else 0))
        stores = [(res, table) for _, _, res, table in sinks if table is not None]
        with nc.Block() as block:
            @block.sync
            def _(sp):
                for k, wd in enumerate(w_drams):
                    s_, c0 = wd[1], wd[2]
                    sp.dma_start(w[:, s_, :, c0:c0 + wd[0].shape[1]], by_partition(wd[0])).then_inc(w_in, 16)
                if bias is not None:
                    sp.dma_start(brow[:, 0:cols], bias.rearrange("(a n) -> a n", a=1)).then_inc(w_in, 16)
                if stores:
                    with nc.sync.Fori(0, NT // CH) as i:
                        sp.wait_ge(evacuated, i * CH + CH)
                        for res, table in stores:
                            sp.dma_start(tile_rows(table[ds(i * (CH * P), CH * P), :]),
                                         res[:, ds(i * CH, CH), :]).then_inc(stored, 16)
                    sp.wait_ge(stored, 16 * len(stores) * (NT // CH))

            @block.vector
            def _(dve):
                v = nc.vector
                v.memset(one[:], 1.0).then_inc(one_set, 1)
                per = 2 * CH + 1 + (xn is not None) if ln else 0
                with nc.vector.Fori(0, NT // CH) as i:
                    o = Order(dve, own, i * per)
                    if ln:
                        dve.wait_ge(rows_set, i * CH)
                        for j in range(CH):
                            o.then(v.bn_stats(stats[:, j, :], srcs[0][:, ds(i * CH + j, 1), :].rearrange("p a d -> p (a d)")))
                        o.wait()
                        dve.sem_inc(passed, 1)
                        for j in range(CH):
                            o.then(v.bn_aggr(mv[:, j, :], stats[:, j, :]))
                        o.wait()
                        v.tensor_scalar(veps[:], mv[:, :, 1], 1e-5, None, ALU.add).then_inc(var_set, 1)
                        dve.wait_ge(std_set, i + 1)
                        o.link(v.reciprocal(rstd[:], std[:]))
                    dve.wait_ge(turned, i * CH)
                    for j in range(CH):
                        for s_ in range(S):
                            at = srcs[s_][:, ds(i * CH + j, 1), :].rearrange("p a d -> p (a d)")
                            if ln:
                                ins = v.tensor_scalar(rows[:, j, s_, :], at, mv[:, j, 0:1], rstd[:, j:j + 1],
                                                      ALU.subtract, ALU.mult)
                            else:
                                ins = v.tensor_copy(rows[:, j, s_, :], at)
                        ins.then_inc(rows_set, 1)
                    if ln and xn is not None:
                        dve.wait_ge(rows_set, i * CH + CH)
                        o.then(v.tensor_copy(xn[:, ds(i * CH, CH), :], rows[:, :, 0, :]))
                    for j in range(CH) if cols else ():
                        dve.wait_ge(multiplied, i * CH + j + 1)
                        for k, (c0, c1, res, _) in enumerate(sinks):
                            out = res[:, ds(i * CH + j, 1), :].rearrange("p a d -> p (a d)")
                            b = (j % DEPTH) * NB + c0 // 512
                            inp = ps_o[:, b, c0 % 512:c0 % 512 + c1 - c0]
                            if relu_add is not None:
                                ins = v.scalar_tensor_tensor(out, inp, 0.0, out, ALU.max, ALU.add)
                            else:
                                ins = v.tensor_copy(out, inp)
                        ins.then_inc(evacuated, 1)

            @block.tensor
            def _(pe):
                if WL:
                    pe.wait_ge(w_in, WL)
                pe.wait_ge(one_set, 1)
                with nc.tensor.Fori(0, NT // CH) as i:
                    def turn(j):
                        pe.wait_ge(rows_set, i * CH + j + 1)
                        pe.wait_ge(taken, i * CH + max(j - 1, 0))
                        for s_ in range(S):
                            for k in range(KD):
                                q = s_ * KD + k
                                ins = nc.tensor.transpose(ps_t[:, j % 2, q * P:(q + 1) * P],
                                                          rows[:, j, s_, k * P:(k + 1) * P], g.ident[:])
                        ins.then_inc(turned, 1)

                    turn(0)
                    for j in range(CH):
                        if j + 1 < CH:
                            turn(j + 1)
                        if not cols:
                            continue
                        pe.wait_ge(taken, i * CH + j + 1)
                        pe.wait_ge(evacuated, i * CH + max(j - DEPTH + 1, 0))
                        for b in range(NB):
                            c0, c1 = b * 512, min(cols, b * 512 + 512)
                            out = ps_o[:, (j % DEPTH) * NB + b, 0:c1 - c0]
                            for q in range(S * KD):
                                ins = nc.tensor.matmul(out, rows_t[:, j, q, :], w[:, q // KD, q % KD, c0:c1],
                                                       start=q == 0, stop=bias is None and q == S * KD - 1)
                            if bias is not None:
                                ins = nc.tensor.matmul(out, one[:], brow[:, c0:c1], start=False, stop=True)
                        ins.then_inc(multiplied, 1)

            @block.scalar
            def _(act):
                with nc.scalar.Fori(0, NT // CH) as i:
                    if ln:
                        act.wait_ge(var_set, i + 1)
                        nc.scalar.activation(std[:], veps[:], ACT.Sqrt).then_inc(std_set, 1)
                    for j in range(CH):
                        act.wait_ge(turned, i * CH + j + 1)
                        if cols:
                            act.wait_ge(multiplied, i * CH)
                        if xt is not None:
                            ins = nc.scalar.activation(xt[:, :, ds((i * CH + j) * P, P)],
                                                 ps_t[:, j % 2, 0:KD * P].rearrange("p (k n) -> p k n", k=KD), ACT.Copy)
                        if cols:
                            ins = nc.scalar.activation(rows_t[:, j, :, :].rearrange("p q n -> p (q n)"),
                                                       ps_t[:, j % 2, 0:S * KD * P], ACT.Copy)
                        ins.then_inc(taken, 1)


class Gather:

    def __init__(self, nc, ph, g, index, name, width, tables=1):
        self.nc, self.g, self.index, self.width = nc, g, index, width
        self.cols = [ph.sb(f"{name}_cols{b}", [P, HALF], I32) for b in range(2)]
        self.rows = ph.sb(f"{name}_rows", [P, U, width], F32)
        self.got = [ph.sem(f"{name}_got{j}") for j in range(U)]
        self.copied = [ph.sem(f"{name}_copied{b}") for b in range(2)]
        self.used = [ph.sem(f"{name}_used{b}") for b in range(2)]
        self.passed = ph.sem(f"{name}_passed")

    def program(self, pool, table):
        gp = self.nc.gpsimd
        with gp.Fori(0, STEPS // U) as i:
            for b in range(2):
                pool.wait_ge(self.used[b], i)
                gp.tensor_copy(self.cols[b][:], self.index[:, ds(i * U + b * HALF, HALF)]).then_inc(self.copied[b], 1)
                pool.wait_ge(self.copied[b], i + 1)
                pool.sem_inc(self.passed, 1)
                for j in range(HALF):
                    gp.indirect_dma_start(
                        out=self.rows[:, b * HALF + j, :], out_offset=None, in_=table,
                        in_offset=bass.IndirectOffsetOnAxis(ap=self.cols[b][:, j:j + 1], axis=0)
                    ).then_inc(self.got[b * HALF + j], 16)


def edge_sum(nc, g, table, acc, extra, heads=0):
    X = extra.shape[2] if extra is not None else 0
    C = D + X
    with Phase(nc) as ph:
        sb, ps, sem = ph.sb, ph.ps, ph.sem
        ga = Gather(nc, ph, g, g.src_a, "edge", D)
        sel = sb("sel", [P, U, P], F32)
        locs = sb("locs", [P, U], F32)
        wts = sb("wts", [P, U, max(X, 1)], F32)
        msg = sb("msg", [P, U, C], F32) if X else None
        ps_a = ps("ps_a", [P, 8, 512])
        zeroed, own, locs_in, sel_set, msg_set, summed, added = (sem(x) for x in (
            "zeroed", "own", "locs_in", "sel_set", "msg_set", "summed", "added"))
        with nc.Block() as block:
            @block.gpsimd
            def _(pool):
                ga.program(pool, table)

            @block.vector
            def _(dve):
                v = nc.vector
                v.memset(acc[:, :, 0:C], 0.0).then_inc(zeroed, 1)
                dve.wait_ge(zeroed, 1)
                with nc.vector.Fori(0, STEPS // U) as i:
                    tiles = [nc.vector.value_load(g.tile_row[0:1, ds(i * U + j, 1)], min_val=0, max_val=NT - 1) for j in range(U)]
                    dve.wait_ge(summed, i * U)
                    v.tensor_copy(locs[:], g.loc_a[:, ds(i * U, U)]).then_inc(locs_in, 1)
                    if X:
                        v.tensor_copy(wts[:], extra[:, ds(i * U, U), :]).then_inc(locs_in, 1)
                        v.tensor_copy(msg[:, :, D:C], extra[:, ds(i * U, U), :]).then_inc(locs_in, 1)
                        dve.wait_ge(locs_in, i * 3 + 3)
                    else:
                        dve.wait_ge(locs_in, i + 1)
                    for j in range(U):
                        v.tensor_scalar(sel[:, j, :], g.lane[:], locs[:, j:j + 1], None, ALU.is_equal).then_inc(sel_set, 1)

                    def add(j):
                        dve.wait_ge(summed, i * U + j + 1)
                        dve.wait_ge(added, i * U + j)
                        at = acc[:, ds(tiles[j], 1), 0:C].rearrange("p a c -> p (a c)")
                        v.tensor_tensor(at, at, ps_a[:, j % 8, 0:C], ALU.add).then_inc(added, 1)

                    for j in range(U):
                        dve.wait_ge(ga.got[j], i * 16 + 16)
                        if X:
                            if heads == 1:
                                ins = v.tensor_scalar(msg[:, j, 0:D], ga.rows[:, j, :], wts[:, j, 0:1], None, ALU.mult)
                            else:
                                ins = v.tensor_tensor(
                                    msg[:, j, 0:D].rearrange("p (h d) -> p h d", h=heads),
                                    ga.rows[:, j, :].rearrange("p (h d) -> p h d", h=heads),
                                    wts[:, j, 0:heads].unsqueeze(2).broadcast_to([P, heads, D // heads]), ALU.mult)
                            ins.then_inc(msg_set, 1)
                            if j % HALF == HALF - 1:
                                dve.wait_ge(msg_set, i * U + j + 1)
                                dve.sem_inc(ga.used[j // HALF], 1)
                        if j >= 2:
                            add(j - 2)
                    add(U - 2)
                    add(U - 1)

            @block.tensor
            def _(pe):
                with nc.tensor.Fori(0, STEPS // U) as i:
                    for j in range(U):
                        pe.wait_ge(sel_set, i * U + j + 1)
                        pe.wait_ge(added, i * U)
                        if X:
                            pe.wait_ge(msg_set, i * U + j + 1)
                            rhs = msg[:, j, :]
                        else:
                            pe.wait_ge(ga.got[j], i * 16 + 16)
                            rhs = ga.rows[:, j, :]
                        ins = nc.tensor.matmul(ps_a[:, j % 8, 0:C], sel[:, j, :], rhs, start=True, stop=True)
                        ins.then_inc(summed, 1)
                        if not X and j % HALF == HALF - 1:
                            pe.wait_ge(summed, i * U + j + 1)
                            pe.sem_inc(ga.used[j // HALF], 1)


def edge_logits(nc, g, table, width, node_cols, logits, second=None, attr_w=None, dot_scale=None):
    W = node_cols.shape[2]
    H = logits.shape[2]
    with Phase(nc) as ph:
        sb, ps, sem = ph.sb, ph.ps, ph.sem
        ga = Gather(nc, ph, g, g.src_a, "logit", width)
        locs = sb("locs", [P, 2, HALF * P], BF16)
        sel_t = sb("sel_t", [P, U, P], F32)
        att = sb("att", [EA, U, P], F32) if attr_w is not None else None
        total = sb("total", [P, 2, HALF, H], F32)
        prod = sb("prod", [P, 2, D], F32)
        ps_b = ps("ps_b", [P, 2, 2 if W > P else 1, 512])
        locs_in = [sem(f"locs_in{b}") for b in range(2)]
        sel_set = [sem(f"sel_set{b}") for b in range(2)]
        made = [sem(f"made{b}") for b in range(2)]
        read = [sem(f"read{b}") for b in range(2)]
        att_in = [sem(f"att_in{j}") for j in range(U)] if attr_w is not None else None
        own = sem("own")

        def product(b, j):
            if W > P:
                return ps_b[:, b, j // 2, (j % 2) * 256:(j % 2) * 256 + W]
            return ps_b[:, b, 0, j * P:j * P + W]

        with nc.Block() as block:
            @block.gpsimd
            def _(pool):
                ga.program(pool, table)

            @block.sync
            def _(sp):
                with nc.sync.Fori(0, STEPS // U) as i:
                    for b in range(2):
                        sp.wait_ge(sel_set[b], i)
                        sp.dma_start(locs[:, b, :], g.loc_slots[ds(i * (U * P) + b * HALF * P, HALF * P)]
                                     .partition_broadcast(P)).then_inc(locs_in[b], 16)
                        if attr_w is not None:
                            sp.wait_ge(made[b], i)
                            for j in range(b * HALF, (b + 1) * HALF):
                                r = nc.sync.value_load(g.row_row[0:1, ds(i * U + j, 1)], min_val=0, max_val=ROWS - 1)
                                sp.dma_start(att[:, j, :], g.ins["attr_t"][ds(r, 1), :, :].rearrange("a e l -> (a e) l")
                                             ).then_inc(att_in[j], 16)

            @block.vector
            def _(dve):
                v = nc.vector
                n = HALF + 1 if dot_scale else 1
                with nc.vector.Fori(0, STEPS // U) as i:
                    for b in range(2):
                        dve.wait_ge(locs_in[b], i * 16 + 16)
                        dve.wait_ge(made[b], i)
                        v.tensor_scalar(sel_t[:, b * HALF:(b + 1) * HALF, :].rearrange("p j e -> p (j e)"), locs[:, b, :],
                                        g.pidx[:], None, ALU.is_equal).then_inc(sel_set[b], 1)
                    o = Order(dve, own, i * (2 * n))
                    for b in range(2):
                        at = logits[:, ds(i * U + b * HALF, HALF), :]
                        dve.wait_ge(made[b], i + 1)
                        dve.wait_ge(read[b], i)
                        for j in range(b * HALF, (b + 1) * HALF):
                            dve.wait_ge(ga.got[j], i * 16 + 16)
                        if dot_scale:
                            for j in range(HALF):
                                if b or j:
                                    o.wait()
                                o.then(v.tensor_tensor_reduce(prod[:, 0, :], ga.rows[:, b * HALF + j, :], product(b, j),
                                                              dot_scale, 0.0, ALU.mult, ALU.add, total[:, b, j, :]))
                            o.wait()
                            o.then(v.tensor_copy(at, total[:, b, :, :]))
                            o.wait()
                            dve.sem_inc(read[b], 1)
                        else:
                            both = ps_b[:, b, 0, :].rearrange("p (j c) -> p j c", c=P)
                            o.link(v.tensor_tensor(total[:, b, :, :], ga.rows[:, b * HALF:(b + 1) * HALF, :],
                                                   both[:, :, 0:H], ALU.add))
                            if second is not None:
                                v.tensor_copy(second[:, ds(i * U + b * HALF, HALF), :], both[:, :, H:2 * H])
                            v.scalar_tensor_tensor(at, total[:, b, :, :], 0.2, total[:, b, :, :], ALU.mult, ALU.max
                                                   ).then_inc(read[b], 1)
                        dve.wait_ge(read[b], i + 1)
                        dve.sem_inc(ga.used[b], 1)

            @block.tensor
            def _(pe):
                with nc.tensor.Fori(0, STEPS // U) as i:
                    for b in range(2):
                        pe.wait_ge(sel_set[b], i + 1)
                        pe.wait_ge(read[b], i)
                        for j in range(HALF):
                            q = b * HALF + j
                            n = nc.tensor.value_load(g.tile_row[0:1, ds(i * U + q, 1)], min_val=0, max_val=NT - 1)
                            ins = nc.tensor.matmul(product(b, j), sel_t[:, q, :],
                                                   node_cols[:, ds(n, 1), :].rearrange("p a c -> p (a c)"),
                                                   start=True, stop=attr_w is None)
                            if attr_w is not None:
                                pe.wait_ge(att_in[q], i * 16 + 16)
                                ins = nc.tensor.matmul(product(b, j), att[:, q, :], attr_w, start=False, stop=True)
                        ins.then_inc(made[b], 1)


def segment_max(nc, g, logits, maxima, H):
    G = {8: 16, 4: 32, 1: SPG}[H]
    GH, NG = G * H, STEPS // G
    with Phase(nc) as ph:
        sb, ps, sem = ph.sb, ph.ps, ph.sem
        lt = sb("lt", [P, G, H], F32)
        dt = sb("dt", [P, G, H], F32)
        lb = sb("lb", [GH, NG, P], F32)
        ne = sb("ne", [GH, NG, P + 1], F32)
        db = sb("db", [GH, P], F32)
        lq = sb("lq", [GH, P], F32)
        nq = sb("nq", [GH, P + 1], F32)
        fwd = sb("fwd", [GH, P], F32)
        bwd = sb("bwd", [GH, P], F32)
        ends = sb("ends", [GH, 2, NG], F32)
        rows = sb("rows", [1, 2, STEPS, H], F32)
        over = sb("over", [1, 2, STEPS], F32)
        given = sb("given", [1, 2, STEPS, H], F32)
        dlast = sb("dlast", [1, STEPS], F32)
        cut = sb("cut", [1, STEPS + 1], F32)
        part = sb("part", [1, STEPS], F32)
        reset = sb("reset", [1, 2, STEPS], F32)
        given_b = sb("given_b", [GH, 2, NG], F32)
        start = sb("start", [GH, 2], F32)
        top = sb("top", [GH, P], F32)
        ps_x = ps("ps_x", [P, 2, 512])
        ps_y = ps("ps_y", [P, P])
        own, laid, turned, read, kept, found, dma, carried, topped, back, taken = (sem(x) for x in (
            "own", "laid", "turned", "read", "kept", "found", "dma", "carried", "topped", "back", "taken"))
        with nc.Block() as block:
            @block.vector
            def _(dve):
                v = nc.vector
                o = Order(dve, own)
                o.link(v.memset(nq[:], 0.0))
                NA = 8
                with nc.vector.Fori(0, NG) as q:
                    o = Order(dve, own, q * NA + 1)
                    dve.wait_ge(turned, q)
                    v.tensor_copy(lt[:], logits[:, ds(q * G, G), :]).then_inc(laid, 1)
                    v.tensor_copy(dt[:], g.dst_a[:, ds(q * G, G)].unsqueeze(2).broadcast_to([P, G, H])).then_inc(laid, 1)
                    dve.wait_ge(turned, q + 1)
                    o.link(v.tensor_copy(db[:], ps_x[0:GH, 1, 0:P]))
                    o.link(v.tensor_tensor(nq[:, 1:P], db[:, 1:P], db[:, 0:P - 1], ALU.not_equal))
                    o.link(v.tensor_scalar(nq[:, 1:P], nq[:, 1:P], -BIG, None, ALU.mult))
                    dve.wait_ge(kept, q + 1)
                    o.then(v.tensor_copy(ne[:, ds(q, 1), :].rearrange("p a l -> p (a l)"), nq[:]))
                    o.link(v.tensor_tensor_scan(fwd[:], nq[:, 0:P], lq[:], -BIG, ALU.add, ALU.max))
                    o.then(v.tensor_tensor_scan(bwd[:], nq[:, P:0:-1], lq[:, ::-1], -BIG, ALU.add, ALU.max))
                    o.then(v.tensor_copy(ends[:, 0, ds(q, 1)], fwd[:, P - 1:P]))
                    o.wait()
                    o.link(v.tensor_copy(ends[:, 1, ds(q, 1)], bwd[:, P - 1:P]))
                    dve.sem_inc(read, 1)
                dve.sem_inc(found, 1)
                o = Order(dve, own, NG * NA + 1)
                dve.wait_ge(dma, 16)
                dfirst = g.dst_a[0:1, :]
                o.then(v.memset(cut[:], -BIG))
                o.link(v.tensor_tensor(part[:], dfirst, dlast[:], ALU.not_equal))
                o.link(v.tensor_scalar(part[:], part[:], -BIG, None, ALU.mult))
                o.link(v.tensor_tensor(cut[:, 1:STEPS], dfirst[:, 1:STEPS], dlast[:, 0:STEPS - 1], ALU.not_equal))
                o.link(v.tensor_scalar(cut[:, 1:STEPS], cut[:, 1:STEPS], -BIG, None, ALU.mult))
                o.then(v.tensor_tensor(reset[:, 0, :], part[:], cut[:, 0:STEPS], ALU.min))
                o.then(v.tensor_tensor(reset[:, 1, :], part[:], cut[:, 1:STEPS + 1], ALU.min))
                o.then(v.memset(given[:], -BIG))
                o.wait()
                dve.wait_ge(dma, 80)
                for h in range(H):
                    o.then(v.tensor_tensor_scan(over[:, 0, :], reset[:, 0, :], rows[:, 0, :, h], -BIG, ALU.add, ALU.max))
                    o.link(v.tensor_tensor_scan(over[:, 1, ::-1], reset[:, 1, ::-1], rows[:, 1, ::-1, h], -BIG, ALU.add, ALU.max))
                    o.then(v.tensor_tensor(given[:, 0, 1:STEPS, h], over[:, 0, 0:STEPS - 1], cut[:, 1:STEPS], ALU.add))
                    o.link(v.tensor_tensor(given[:, 1, 0:STEPS - 1, h], over[:, 1, 1:STEPS], cut[:, 1:STEPS], ALU.add))
                dve.sem_inc(carried, 1)
                dve.wait_ge(dma, 144)
                base = o.at
                with nc.vector.Fori(0, NG) as q:
                    o = Order(dve, own, q * 6 + base)
                    o.then(v.tensor_copy(nq[:], ne[:, ds(q, 1), :].rearrange("p a l -> p (a l)")))
                    o.then(v.tensor_copy(lq[:], lb[:, ds(q, 1), :].rearrange("p a l -> p (a l)")))
                    o.link(v.tensor_copy(start[:], given_b[:, :, ds(q, 1)].rearrange("p c a -> p (c a)")))
                    o.then(v.tensor_tensor_scan(fwd[:], nq[:, 0:P], lq[:], start[:, 0:1], ALU.add, ALU.max))
                    o.link(v.tensor_tensor_scan(bwd[:, ::-1], nq[:, P:0:-1], lq[:, ::-1], start[:, 1:2], ALU.add, ALU.max))
                    dve.wait_ge(back, q)
                    o.link(v.tensor_tensor(top[:], fwd[:], bwd[:], ALU.max))
                    dve.sem_inc(topped, 1)

            @block.tensor
            def _(pe):
                with nc.tensor.Fori(0, NG) as q:
                    pe.wait_ge(laid, q * 2 + 2)
                    pe.wait_ge(read, q)
                    pe.wait_ge(kept, q)
                    nc.tensor.transpose(ps_x[0:GH, 0, 0:P], lt[:].rearrange("p g h -> p (g h)"), g.ident[:])
                    nc.tensor.transpose(ps_x[0:GH, 1, 0:P], dt[:].rearrange("p g h -> p (g h)"), g.ident[:]).then_inc(turned, 1)
                with nc.tensor.Fori(0, NG) as q:
                    pe.wait_ge(topped, q + 1)
                    pe.wait_ge(taken, q)
                    nc.tensor.transpose(ps_y[:, 0:GH], top[:], g.ident[0:GH, 0:GH]).then_inc(back, 1)

            @block.scalar
            def _(act):
                with nc.scalar.Fori(0, NG) as q:
                    act.wait_ge(turned, q + 1)
                    act.wait_ge(read, q)
                    nc.scalar.activation(lb[:, ds(q, 1), :].rearrange("p a l -> p (a l)"), ps_x[0:GH, 0, 0:P],
                                         ACT.Copy)
                    nc.scalar.activation(lq[:], ps_x[0:GH, 0, 0:P], ACT.Copy).then_inc(kept, 1)
                with nc.scalar.Fori(0, NG) as q:
                    act.wait_ge(back, q + 1)
                    nc.scalar.activation(maxima[:, ds(q * G, G), :].rearrange("p g h -> p (g h)"), ps_y[:, 0:GH],
                                         ACT.Copy).then_inc(taken, 1)

            @block.sync
            def _(sp):
                seg = g.seg_dram
                sp.dma_start(dlast[:], g.dst_a[P - 1:P, :]).then_inc(dma, 16)
                sp.wait_ge(found, 1)
                sp.wait_ge(dma, 16)
                with nc.allow_non_contiguous_dma("4-byte elements: a few thousand"):
                    for c in range(2):
                        sp.dma_start(seg[c, 0:STEPS * H].rearrange("(q p) -> p q", p=GH), ends[:, c, :]).then_inc(dma, 16)
                    sp.wait_ge(dma, 48)
                    for c in range(2):
                        sp.dma_start(rows[:, c, :, :].rearrange("a k h -> a (k h)"),
                                     seg[c:c + 1, 0:STEPS * H]).then_inc(dma, 16)
                    sp.wait_ge(carried, 1)
                    sp.wait_ge(dma, 80)
                    for c in range(2):
                        sp.dma_start(seg[2 + c:3 + c, 0:STEPS * H],
                                     given[:, c, :, :].rearrange("a k h -> a (k h)")).then_inc(dma, 16)
                    sp.wait_ge(dma, 112)
                    for c in range(2):
                        sp.dma_start(given_b[:, c, :], seg[2 + c, 0:STEPS * H].rearrange("(q p) -> p q", p=GH)).then_inc(dma, 16)
                    sp.wait_ge(dma, 144)


def bulk(nc, steps, loads=()):
    with Phase(nc) as ph:
        turn, loaded = ph.sem("turn"), ph.sem("loaded")
        with nc.Block() as block:
            @block.sync
            def _(sp):
                for out, in_ in loads:
                    sp.dma_start(out, in_).then_inc(loaded, 16)
                if loads:
                    sp.wait_ge(loaded, 16 * len(loads))

            @block.vector
            def _(dve):
                if loads:
                    dve.wait_ge(loaded, 16 * len(loads))
                for n, (who, make) in enumerate(steps):
                    if who == "v":
                        if n:
                            dve.wait_ge(turn, n)
                        make(nc.vector).then_inc(turn, 1)

            @block.scalar
            def _(act):
                if loads:
                    act.wait_ge(loaded, 16 * len(loads))
                for n, (who, make) in enumerate(steps):
                    if who == "a":
                        if n:
                            act.wait_ge(turn, n)
                        make(nc.scalar).then_inc(turn, 1)


def turn_weights(nc, g, wts, wts_t):
    with Phase(nc) as ph:
        fixed = ph.sb("fixed", [P, CH, NE], F32)
        ps_w = ph.ps("ps_w", [P, 2, 512])
        laid, turned, taken = ph.sem("laid"), ph.sem("turned"), ph.sem("taken")
        with nc.Block() as block:
            @block.vector
            def _(dve):
                with nc.vector.Fori(0, NT // CH) as i:
                    dve.wait_ge(turned, i)
                    nc.vector.tensor_copy(fixed[:], wts[:, ds(i * CH, CH), :]).then_inc(laid, 1)

            @block.tensor
            def _(pe):
                with nc.tensor.Fori(0, NT // CH) as i:
                    pe.wait_ge(laid, i + 1)
                    pe.wait_ge(taken, i * 2)
                    for j in range(CH):
                        ins = nc.tensor.transpose(ps_w[0:NE, j // 4, (j % 4) * P:(j % 4 + 1) * P], fixed[:, j, :], g.ident[:])
                    ins.then_inc(turned, 1)

            @block.scalar
            def _(act):
                with nc.scalar.Fori(0, NT // CH) as i:
                    act.wait_ge(turned, i + 1)
                    nc.scalar.activation(wts_t[:, ds(i * TOK, 512)], ps_w[0:NE, 0, :], ACT.Copy).then_inc(taken, 1)
                    nc.scalar.activation(wts_t[:, ds(i * TOK + 512, P)], ps_w[0:NE, 1, 0:P], ACT.Copy).then_inc(taken, 1)


def experts(nc, g, xt, hidden, w_last, b_last, wts, wts_t):
    L = len(hidden)
    dims = [D] + [h[0].shape[2] for h in hidden] + [w_last.shape[2]]
    HF = TOK // 2
    order = []
    for t in range(NE + L):
        for s_ in range(L, -1, -1):
            if 0 <= t - s_ < NE:
                order.append((t - s_, s_))
    inner = [(e, l, m, h) for e, l in order if l < L for m in range(dims[l + 1] // P) for h in range(2)]
    outer = [(e, t) for e, l in order if l == L for t in range(CH)] + [(NE, t) for t in range(CH)]
    at = {k: n for n, k in enumerate(inner)}
    done = {(e, l): at[(e, l, dims[l + 1] // P - 1, 1)] + 1 for e, l in order if l < L}
    out_at = {k: n for n, k in enumerate(outer)}
    NI, NO = len(inner), len(outer)
    with Phase(nc) as ph:
        sb, ps, sem = ph.sb, ph.ps, ph.sem
        ws = [sb(f"w{l}", [P, NE, dims[l] // P, dims[l + 1]], F32) for l in range(L + 1)]
        hid = [sb(f"hid{l}", [P, 2, dims[l + 1] // P, TOK], F32) for l in range(L)]
        b_out = sb("b_out", [NE, D], F32)
        wc = sb("wc", [P, CH, NE], F32)
        wtc = sb("wtc", [NE, TOK], F32)
        y = sb("y", [P, CH, D], F32)
        ps_h = ps("ps_h", [P, 4, 512])
        ps_y = ps("ps_y", [P, 4, 512])
        w_in = [sem(f"w_in{e}") for e in range(NE)]
        b_in, made, shaped, made_y, added, stored, wc_in, wt_in = (sem(x) for x in (
            "b_in", "made", "shaped", "made_y", "added", "stored", "wc_in", "wt_in"))
        with nc.Block() as block:
            @block.sync
            def _(sp):
                sp.dma_start(b_out[:], b_last).then_inc(b_in, 16)
                for e in range(NE):
                    for l in range(L + 1):
                        wd = hidden[l][0] if l < L else w_last
                        sp.dma_start(ws[l][:, e, :, :], by_partition(wd[e])).then_inc(w_in[e], 16)
                for e in range(NE):
                    sp.wait_ge(w_in[e], 16 * (L + 1))

            @block.tensor
            def _(pe):
                with nc.tensor.Fori(0, NT // CH) as i:
                    def inner_layer(e, l):
                        if l == 0:
                            pe.wait_ge(w_in[e], 16 * (L + 1))
                        else:
                            pe.wait_ge(shaped, i * NI + done[(e, l - 1)])
                        for m in range(dims[l + 1] // P):
                            for h in range(2):
                                n = at[(e, l, m, h)]
                                pe.wait_ge(shaped, i * NI + max(n - 3, 0))
                                K = dims[l] // P
                                for k in range(K):
                                    rhs = (xt[:, k, ds(i * TOK + h * HF, HF)] if l == 0
                                           else hid[l - 1][:, e % 2, k, h * HF:(h + 1) * HF])
                                    ins = nc.tensor.matmul(ps_h[:, n % 4, 0:HF], ws[l][:, e, k, m * P:(m + 1) * P], rhs,
                                                           start=k == 0, stop=k == K - 1)
                                ins.then_inc(made, 1)

                    def outer_layer(e):
                        if e < NE:
                            pe.wait_ge(shaped, i * NI + done[(e, L - 1)])
                        else:
                            pe.wait_ge(wt_in, i + 1)
                            pe.wait_ge(b_in, 16)
                        for t in range(CH):
                            n = out_at[(e, t)]
                            pe.wait_ge(added, i * NO + max(n - 3, 0))
                            if e == NE:
                                ins = nc.tensor.matmul(ps_y[:, n % 4, 0:D], wtc[:, t * P:(t + 1) * P], b_out[:],
                                                       start=True, stop=True)
                            else:
                                K = dims[L] // P
                                for k in range(K):
                                    ins = nc.tensor.matmul(ps_y[:, n % 4, 0:D], hid[L - 1][:, e % 2, k, t * P:(t + 1) * P],
                                                           ws[L][:, e, k, :], start=k == 0, stop=k == K - 1)
                            ins.then_inc(made_y, 1)

                    for e, l in order:
                        if l < L:
                            inner_layer(e, l)
                        else:
                            outer_layer(e)
                    outer_layer(NE)

            @block.scalar
            def _(act):
                with nc.scalar.Fori(0, NT // CH) as i:
                    act.wait_ge(made_y, i * NO)
                    nc.scalar.activation(wtc[:], wts_t[:, ds(i * TOK, TOK)], ACT.Copy).then_inc(wt_in, 1)
                    for n, (e, l, m, h) in enumerate(inner):
                        act.wait_ge(made, i * NI + n + 1)
                        if l == L - 1:
                            act.wait_ge(made_y, i * NO + (out_at[(e - 2, CH - 1)] + 1 if e >= 2 else 0))
                        _, func, scales, biases = hidden[l]
                        nc.scalar.activation(hid[l][:, e % 2, m, h * HF:(h + 1) * HF], ps_h[:, n % 4, 0:HF], func,
                                             bias=biases[:, e, m:m + 1],
                                             scale=scales[:, e, m:m + 1] if scales is not None else 1.0).then_inc(shaped, 1)

            @block.vector
            def _(dve):
                v = nc.vector
                with nc.vector.Fori(0, NT // CH) as i:
                    dve.wait_ge(added, i * NO)
                    v.tensor_copy(wc[:], wts[:, ds(i * CH, CH), :]).then_inc(wc_in, 1)
                    dve.wait_ge(wc_in, i + 1)
                    dve.wait_ge(stored, i)
                    for n, (e, t) in enumerate(outer):
                        dve.wait_ge(made_y, i * NO + n + 1)
                        if e:
                            dve.wait_ge(added, i * NO + out_at[(e - 1, t)] + 1)
                        src = ps_y[:, n % 4, 0:D]
                        if e == 0:
                            ins = v.tensor_scalar(y[:, t, :], src, wc[:, t, e:e + 1], None, ALU.mult)
                        elif e < NE:
                            ins = v.scalar_tensor_tensor(y[:, t, :], src, wc[:, t, e:e + 1], y[:, t, :], ALU.mult, ALU.add)
                        else:
                            ins = v.tensor_tensor(y[:, t, :], src, y[:, t, :], ALU.add)
                        ins.then_inc(added, 1)
                    dve.wait_ge(added, i * NO + NO)
                    xs = g.x[:, ds(i * CH, CH), :]
                    v.tensor_tensor(xs, xs, y[:], ALU.add).then_inc(stored, 1)


def head_dots(rows, att, tmp, out, H):
    return [("v", lambda v: v.tensor_tensor(tmp, rows, att.unsqueeze(1).broadcast_to([P, NT, D]), ALU.mult)),
            ("v", lambda v: v.tensor_reduce(out, tmp.rearrange("p t (h d) -> p t h d", h=H), AX_X, ALU.add))]


def to_dram(nc, pairs):
    with Phase(nc) as ph:
        out = ph.sem("out")
        with nc.Block() as block:
            @block.sync
            def _(sp):
                for to, of in pairs:
                    sp.dma_start(to, of).then_inc(out, 16)
                sp.wait_ge(out, 16 * len(pairs))


def row_bc(ap, parts=P):
    return ap.partition_broadcast(parts)


def gnn0(nc, g):
    with Phase(nc) as ph:
        sb = ph.sb
        logits = sb("logits", [P, STEPS, 8], F32)
        wee = sb("wee", [EA, 8], F32)
        et = sb("et", [P, NT, 8], F32)
        with Phase(nc) as p2:
            ft = p2.sb("ft", [P, NT, D], F32)
            tmp = p2.sb("tmp", [P, NT, D], F32)
            eh = p2.sb("eh", [P, NT, 8], F32)
            ath, att, ate = (p2.sb(n, [P, D], F32) for n in ("ath", "att", "ate"))
            we = p2.sb("we", [EA, D], F32)
            node_rows(nc, g, [g.x], [(g.ins["L0_gnn_W_fc"], 0, 0)], D, None, [(0, D, ft, g.tab)], ln=True)
            bulk(nc, head_dots(ft[:], ath[:], tmp[:], eh[:], 8) + head_dots(ft[:], att[:], tmp[:], et[:], 8) + [
                ("v", lambda v: v.tensor_mul(we[:], we[:], ate[0:EA, :])),
                ("v", lambda v: v.tensor_reduce(wee[:], we[:].rearrange("p (h d) -> p h d", h=8), AX_X, ALU.add))],
                loads=[(ath[:], row_bc(g.ins["L0_gnn_attn_h"])), (att[:], row_bc(g.ins["L0_gnn_attn_t"])),
                       (ate[:], row_bc(g.ins["L0_gnn_attn_e"])), (we[:], g.ins["L0_gnn_W_e"])])
            to_dram(nc, [(tile_rows(g.tab8), eh[:])])
        edge_logits(nc, g, g.tab8, 8, et, logits, attr_w=wee[:])
        with Phase(nc) as p2:
            maxima = p2.sb("maxima", [P, STEPS, 8], F32)
            segment_max(nc, g, logits, maxima, 8)
            bulk(nc, [("v", lambda v: v.tensor_sub(logits[:], logits[:], maxima[:])),
                      ("a", lambda a: a.activation(logits[:], logits[:], ACT.Exp))])
        acc = sb("acc", [P, NT, AC], F32)
        edge_sum(nc, g, g.tab, acc, logits, heads=8)
        bias = sb("bias", [P, D], F32)
        den = acc[:, :, D:D + 8]
        feat = acc[:, :, 0:D]
        bulk(nc, [("v", lambda v: v.tensor_scalar(den, den, 1e-20, None, ALU.max)),
                  ("v", lambda v: v.reciprocal(den, den)),
                  ("v", lambda v: v.tensor_tensor(feat.rearrange("p t (h d) -> p t h d", h=8),
                                                  feat.rearrange("p t (h d) -> p t h d", h=8),
                                                  den.unsqueeze(3).broadcast_to([P, NT, 8, 32]), ALU.mult)),
                  ("v", lambda v: v.tensor_add(g.x[:], g.x[:], feat)),
                  ("v", lambda v: v.tensor_tensor(g.x[:], g.x[:], bias[:].unsqueeze(1).broadcast_to([P, NT, D]), ALU.add))],
             loads=[(bias[:], row_bc(g.ins["L0_gnn_bias"]))])


def softmax8(w, top, tot):
    bc = lambda a: a.unsqueeze(2).broadcast_to([P, NT, NE])
    return [("v", lambda v: v.tensor_reduce(top, w, AX_X, ALU.max)),
            ("v", lambda v: v.tensor_tensor(w, w, bc(top), ALU.subtract)),
            ("a", lambda a: a.activation(w, w, ACT.Exp)),
            ("v", lambda v: v.tensor_reduce(tot, w, AX_X, ALU.add)),
            ("v", lambda v: v.reciprocal(tot, tot)),
            ("v", lambda v: v.tensor_tensor(w, w, bc(tot), ALU.mult))]


def ffn0(nc, g):
    with Phase(nc) as ph:
        sb = ph.sb
        xt = sb("xt", [P, KD, NP_], F32)
        w = sb("w", [P, NT, NE], F32)
        wt = sb("wt", [NE, NP_], F32)
        top, tot = sb("top", [P, NT], F32), sb("tot", [P, NT], F32)
        vec = [sb(f"vec{q}", [P, 5, NE, KD], F32) for q in range(2)]
        node_rows(nc, g, [g.x], [(g.ins["L0_ffn_Wr"], 0, 0)], NE, g.ins["L0_ffn_br"], [(0, NE, w, None)], ln=True, xt=xt)
        steps = softmax8(w[:], top[:], tot[:])
        for q in range(2):
            b, ga, be, m, va = (vec[q][:, c, :, :] for c in range(5))
            steps += [("v", lambda v, va=va: v.tensor_scalar(va, va, 1e-3, None, ALU.add)),
                      ("a", lambda a, va=va: a.activation(va, va, ACT.Sqrt)),
                      ("v", lambda v, va=va: v.reciprocal(va, va)),
                      ("v", lambda v, va=va, ga=ga: v.tensor_mul(ga, ga, va)),
                      ("v", lambda v, b=b, m=m: v.tensor_sub(b, b, m)),
                      ("v", lambda v, b=b, ga=ga: v.tensor_mul(b, b, ga)),
                      ("v", lambda v, b=b, be=be: v.tensor_add(b, b, be))]
        bulk(nc, steps, loads=[(vec[q][:], (g.ins["L0_ffn_vec1"], g.ins["L0_ffn_vec2"])[q]) for q in range(2)])
        turn_weights(nc, g, w, wt)
        experts(nc, g, xt, [(g.ins["L0_ffn_W1"], ACT.Relu, vec[0][:, 1, :, :], vec[0][:, 0, :, :]),
                            (g.ins["L0_ffn_W2"], ACT.Relu, vec[1][:, 1, :, :], vec[1][:, 0, :, :])],
                g.ins["L0_ffn_Wo"], g.ins["L0_ffn_bo"], w, wt)


def top2(nc, g, w, bias_rows=()):
    with Phase(nc) as ph:
        sb = ph.sb
        iota = sb("iota", [P, NE], F32)
        eq, oh, rest = (sb(n, [P, NT, NE], F32) for n in ("eq", "oh", "rest"))
        oh2 = sb("oh2", [P, NT, NE], F32)
        m1, m2, idx, w0 = (sb(n, [P, NT], F32) for n in ("m1", "m2", "idx", "w0"))
        rows = [sb(f"row{n}", [P, NE], F32) for n in range(len(bias_rows))]
        bc = lambda a: a.unsqueeze(2).broadcast_to([P, NT, NE])
        across = lambda a: a.unsqueeze(1).broadcast_to([P, NT, NE])
        steps = [("v", lambda v: v.tensor_copy(iota[:], g.lane[:, 0:NE]))]
        for r in rows:
            steps.append(("v", lambda v, r=r: v.tensor_tensor(w[:], w[:], across(r[:]), ALU.add)))

        def largest(of, top, hot):
            return [("v", lambda v: v.tensor_reduce(top[:], of, AX_X, ALU.max)),
                    ("v", lambda v: v.tensor_tensor(eq[:], of, bc(top[:]), ALU.is_lt)),
                    ("v", lambda v: v.tensor_scalar(eq[:], eq[:], 100.0, None, ALU.mult)),
                    ("v", lambda v: v.tensor_tensor(eq[:], eq[:], across(iota[:]), ALU.add)),
                    ("v", lambda v: v.tensor_reduce(idx[:], eq[:], AX_X, ALU.min)),
                    ("v", lambda v: v.tensor_tensor(hot[:], across(iota[:]), bc(idx[:]), ALU.is_equal))]

        steps += largest(w[:], m1, oh)
        steps += [("v", lambda v: v.tensor_scalar(rest[:], oh[:], -BIG, None, ALU.mult)),
                  ("v", lambda v: v.tensor_tensor(rest[:], rest[:], w[:], ALU.add))]
        steps += largest(rest[:], m2, oh2)
        steps += [("v", lambda v: v.tensor_sub(m2[:], m2[:], m1[:])),
                  ("a", lambda a: a.activation(m2[:], m2[:], ACT.Exp)),
                  ("v", lambda v: v.tensor_scalar(w0[:], m2[:], 1.0, None, ALU.add)),
                  ("v", lambda v: v.reciprocal(w0[:], w0[:])),
                  ("v", lambda v: v.tensor_mul(m2[:], m2[:], w0[:])),
                  ("v", lambda v: v.tensor_tensor(oh[:], oh[:], bc(w0[:]), ALU.mult)),
                  ("v", lambda v: v.tensor_tensor(oh2[:], oh2[:], bc(m2[:]), ALU.mult)),
                  ("v", lambda v: v.tensor_add(w[:], oh[:], oh2[:]))]
        bulk(nc, steps, loads=[(r[:], row_bc(d)) for r, d in zip(rows, bias_rows)])


def gnn1(nc, g):
    with Phase(nc) as ph:
        sb = ph.sb
        h = sb("h", [P, NT, D], F32)
        acc = sb("acc", [P, NT, AC], F32)
        extra = sb("extra", [P, STEPS, 2], F32)
        with Phase(nc) as p2:
            logits = p2.sb("logits", [P, STEPS, 1], F32)
            maxima = p2.sb("maxima", [P, STEPS, 1], F32)
            q = p2.sb("q", [P, NT, D], F32)
            with Phase(nc) as p3:
                k = p3.sb("k", [P, NT, D], F32)
                v_ = acc[:, :, 0:D]
                node_rows(nc, g, [g.x], [(g.ins["L1_gnn_Wq"], 0, 0), (g.ins["L1_gnn_Wk"], 0, D), (g.ins["L1_gnn_Wv"], 0, 2 * D), (g.ins["L1_gnn_Ws"], 0, 3 * D)],
                          4 * D, g.ins["L1_gnn_b"], [(0, D, q, None), (D, 2 * D, k, g.tab2), (2 * D, 3 * D, v_, g.tab), (3 * D, 4 * D, h, None)],
                          ln=True)
            edge_logits(nc, g, g.tab2, D, q, logits, dot_scale=D ** -0.5)
            segment_max(nc, g, logits, maxima, 1)
            bulk(nc, [("v", lambda v: v.memset(extra[:], 1.0)),
                      ("v", lambda v: v.tensor_sub(logits[:], logits[:], maxima[:])),
                      ("a", lambda a: a.activation(extra[:, :, 0:1], logits[:], ACT.Exp))])
        edge_sum(nc, g, g.tab, acc, extra, heads=1)
        z = sb("z", [P, NT, D], F32)
        rdeg = sb("rdeg", [P, NT], F32)
        al = sb("al", [P, 2], F32)
        gam, bet = sb("gam", [P, 3, D], F32), sb("bet", [P, 3, D], F32)
        feat, den, deg = acc[:, :, 0:D], acc[:, :, D], acc[:, :, D + 1]
        across = lambda a: a.unsqueeze(2).broadcast_to([P, NT, D])
        rows = lambda a: a.unsqueeze(1).broadcast_to([P, NT, D])
        bulk(nc, [("v", lambda v: v.tensor_scalar(den, den, 1e-20, None, ALU.max)),
                  ("v", lambda v: v.reciprocal(den, den)),
                  ("v", lambda v: v.tensor_scalar(rdeg[:], deg, 1.0, None, ALU.max)),
                  ("v", lambda v: v.reciprocal(rdeg[:], rdeg[:])),
                  ("v", lambda v: v.tensor_tensor(feat, feat, across(den), ALU.mult)),
                  ("v", lambda v: v.tensor_add(h[:], h[:], feat)),
                  ("v", lambda v: v.tensor_scalar(h[:], h[:], 0.0, None, ALU.max)),
                  ("a", lambda a: a.activation(al[:, 0:1], al[:, 0:1], ACT.Sigmoid)),
                  ("v", lambda v: v.tensor_scalar(al[:, 1:2], al[:, 0:1], -1.0, 1.0, ALU.mult, ALU.add)),
                  ("v", lambda v: v.tensor_scalar(gam[:], gam[:], float(1.0 / np.sqrt(1.0 + 1e-5)), None, ALU.mult))],
             loads=[(al[:, 0:1], row_bc(g.ins["L1_gnn_alpha_res"])), (gam[:].rearrange("p l d -> p (l d)"), row_bc(g.ins["L1_gnn_gamma"])),
                    (bet[:].rearrange("p l d -> p (l d)"), row_bc(g.ins["L1_gnn_beta"]))])
        for l in range(3):
            to_dram(nc, [(tile_rows(g.tab), h[:])])
            edge_sum(nc, g, g.tab, acc, None)
            bulk(nc, [("v", lambda v: v.tensor_tensor(feat, feat, across(rdeg[:]), ALU.mult))])
            node_rows(nc, g, [feat, h], [(g.ins["L1_gnn_Wl"][l], 0, 0), (g.ins["L1_gnn_Wr"][l], 1, 0)], D, g.ins["L1_gnn_bl"][l], [(0, D, z, None)])
            bulk(nc, [("v", lambda v: v.tensor_tensor(z[:], z[:], rows(gam[:, l, :]), ALU.mult)),
                      ("v", lambda v: v.tensor_tensor(z[:], z[:], rows(bet[:, l, :]), ALU.add)),
                      ("v", lambda v: v.tensor_scalar(h[:], h[:], al[:, 1:2], None, ALU.mult)),
                      ("v", lambda v: v.scalar_tensor_tensor(h[:], z[:], al[:, 0:1], h[:], ALU.mult, ALU.add)),
                      ("v", lambda v: v.tensor_scalar(h[:], h[:], 0.0, None, ALU.max))])
        bulk(nc, [("v", lambda v: v.tensor_add(g.x[:], g.x[:], h[:]))])


def ffn1(nc, g):
    with Phase(nc) as ph:
        sb = ph.sb
        xt = sb("xt", [P, KD, NP_], F32)
        w = sb("w", [P, NT, NE], F32)
        wt = sb("wt", [NE, NP_], F32)
        b1 = sb("b1", [P, NE, 4], F32)
        node_rows(nc, g, [g.x], [(g.ins["L1_ffn_Wg"], 0, 0)], NE, None, [(0, NE, w, None)], ln=True, xt=xt)
        top2(nc, g, w, (g.ins["L1_ffn_bg"], g.ins["L1_ffn_bias"]))
        bulk(nc, [("v", lambda v: v.tensor_copy(b1[:], b1[:]))], loads=[(b1[:], g.ins["L1_ffn_b1"])])
        turn_weights(nc, g, w, wt)
        experts(nc, g, xt, [(g.ins["L1_ffn_W1"], ACT.Relu, None, b1)], g.ins["L1_ffn_W2"], g.ins["L1_ffn_b2"], w, wt)


def gnn2(nc, g):
    with Phase(nc) as ph:
        sb = ph.sb
        hw = sb("hw", [P, NT, D], F32)
        cols = sb("cols", [P, NT, 8], F32)
        a_s = sb("a_s", [P, NT, 4], F32)
        extra = sb("extra", [P, STEPS, 9], F32)
        adst, loop = cols[:, :, 0:4], cols[:, :, 4:8]
        with Phase(nc) as p2:
            tmp = p2.sb("tmp", [P, NT, D], F32)
            ats, atd = p2.sb("ats", [P, D], F32), p2.sb("atd", [P, D], F32)
            node_rows(nc, g, [g.x], [(g.ins["L2_gnn_W"], 0, 0)], D, None, [(0, D, hw, g.tab)], ln=True)
            bulk(nc, head_dots(hw[:], ats[:], tmp[:], a_s[:], 4) + head_dots(hw[:], atd[:], tmp[:], adst, 4) + [
                ("v", lambda v: v.tensor_add(loop, a_s[:], adst)),
                ("v", lambda v: v.scalar_tensor_tensor(loop, loop, 0.2, loop, ALU.mult, ALU.max))],
                loads=[(ats[:], row_bc(g.ins["L2_gnn_att_src"])), (atd[:], row_bc(g.ins["L2_gnn_att_dst"]))])
            to_dram(nc, [(tile_rows(g.tab4), a_s[:])])
        with Phase(nc) as p2:
            logits, shift, loop_e = (p2.sb(n, [P, STEPS, 4], F32) for n in ("logits", "shift", "loop_e"))
            edge_logits(nc, g, g.tab4, 4, cols, logits, second=loop_e)
            segment_max(nc, g, logits, shift, 4)
            one = extra[:, :, 8]
            bulk(nc, [("v", lambda v: v.tensor_tensor(shift[:], shift[:], loop_e[:], ALU.max)),
                      ("v", lambda v: v.tensor_sub(logits[:], logits[:], shift[:])),
                      ("a", lambda a: a.activation(extra[:, :, 0:4], logits[:], ACT.Exp)),
                      ("v", lambda v: v.tensor_scalar(one, g.last_a[:], 0.0, None, ALU.is_ge)),
                      ("v", lambda v: v.tensor_tensor(extra[:, :, 4:8], shift[:], one.unsqueeze(2).broadcast_to([P, STEPS, 4]),
                                                      ALU.mult))])
        acc = sb("acc", [P, NT, AC], F32)
        edge_sum(nc, g, g.tab, acc, extra, heads=4)
        bias = sb("bias", [P, D], F32)
        none = sb("none", [P, NT, 1], F32)
        feat, den, shf, has = acc[:, :, 0:D], acc[:, :, D:D + 4], acc[:, :, D + 4:D + 8], acc[:, :, D + 8:D + 9]
        own = lambda a: a.rearrange("p t (h d) -> p t h d", h=4)
        wide = lambda a: a.unsqueeze(3).broadcast_to([P, NT, 4, 64])
        bulk(nc, [("v", lambda v: v.tensor_scalar(none[:], has, -1.0, 1.0, ALU.mult, ALU.add)),
                  ("v", lambda v: v.tensor_tensor(a_s[:], loop, none[:].broadcast_to([P, NT, 4]), ALU.mult)),
                  ("v", lambda v: v.tensor_add(shf, shf, a_s[:])),
                  ("v", lambda v: v.tensor_sub(loop, loop, shf)),
                  ("a", lambda a: a.activation(loop, loop, ACT.Exp)),
                  ("v", lambda v: v.tensor_add(den, den, loop)),
                  ("v", lambda v: v.reciprocal(den, den)),
                  ("v", lambda v: v.tensor_tensor(own(hw[:]), own(hw[:]), wide(loop), ALU.mult)),
                  ("v", lambda v: v.tensor_add(feat, feat, hw[:])),
                  ("v", lambda v: v.tensor_tensor(own(feat), own(feat), wide(den), ALU.mult)),
                  ("v", lambda v: v.tensor_add(g.x[:], g.x[:], feat)),
                  ("v", lambda v: v.tensor_tensor(g.x[:], g.x[:], bias[:].unsqueeze(1).broadcast_to([P, NT, D]), ALU.add))],
             loads=[(bias[:], row_bc(g.ins["L2_gnn_bias"]))])


def ffn2(nc, g):
    with Phase(nc) as ph:
        sb = ph.sb
        xt = sb("xt", [P, KD, NP_], F32)
        w = sb("w", [P, NT, NE], F32)
        wt = sb("wt", [NE, NP_], F32)
        b1 = sb("b1", [P, NE, KD], F32)
        xn = sb("xn", [P, NT, D], F32)
        node_rows(nc, g, [g.x], [(g.ins["L2_ffn_router_w"], 0, 0)], NE, None, [(0, NE, w, None)], ln=True, xt=xt, xn=xn)
        top2(nc, g, w)
        bulk(nc, [("v", lambda v: v.tensor_add(g.x[:], g.x[:], xn[:]))], loads=[(b1[:], g.ins["L2_ffn_b1"])])
        turn_weights(nc, g, w, wt)
        experts(nc, g, xt, [(g.ins["L2_ffn_w1"], ACT.Gelu, None, b1)], g.ins["L2_ffn_w2"], g.ins["L2_ffn_b2"], w, wt)


def edge_max(nc, g, table, w_dram, acc):
    HP = HALF * P
    with Phase(nc) as ph:
        sb, ps, sem = ph.sb, ph.ps, ph.sem
        ga = Gather(nc, ph, g, g.src_a, "max", D)
        w = sb("w", [EA, D], F32)
        att = sb("att", [EA, U, P], F32)
        same = sb("same", [P, 2, HP], BF16)
        run = sb("run", [P, 2, KD, HP], F32)
        back = sb("back", [P, U, D], F32)
        sel = sb("sel", [P, U, P], F32)
        lasts = sb("lasts", [P, U], F32)
        ps_m = ps("ps_m", [P, 2, KD, 512])
        ps_t = ps("ps_t", [P, 2, 2, D])
        ps_a = ps("ps_a", [P, 2, 2, D])
        att_in = [sem(f"att_in{j}") for j in range(U)]
        same_in = [sem(f"same_in{b}") for b in range(2)]
        w_in, zeroed, made, ran, turned, taken, sel_set, lasts_in, summed, added = (sem(x) for x in (
            "w_in", "zeroed", "made", "ran", "turned", "taken", "sel_set", "lasts_in", "summed", "added"))
        with nc.Block() as block:
            @block.gpsimd
            def _(pool):
                ga.program(pool, table)

            @block.sync
            def _(sp):
                sp.dma_start(w[:], w_dram).then_inc(w_in, 16)
                with nc.sync.Fori(0, STEPS // U) as i:
                    for b in range(2):
                        sp.wait_ge(ran, i * 4 + b * 2 if b else i * 4)
                        sp.dma_start(same[:, b, :], g.same_slots[ds(i * (U * P) + b * HP, HP)].partition_broadcast(P)
                                     ).then_inc(same_in[b], 16)
                        sp.wait_ge(made, i * 2)
                        for j in range(b * HALF, (b + 1) * HALF):
                            r = nc.sync.value_load(g.row_row[0:1, ds(i * U + j, 1)], min_val=0, max_val=ROWS - 1)
                            sp.dma_start(att[:, j, :], g.ins["attr_t"][ds(r, 1), :, :].rearrange("a e l -> (a e) l")
                                         ).then_inc(att_in[j], 16)
                sp.wait_ge(w_in, 16)

            @block.tensor
            def _(pe):
                pe.wait_ge(w_in, 16)
                with nc.tensor.Fori(0, STEPS // U) as i:
                    for b in range(2):
                        pe.wait_ge(ran, i * 4)
                        for j in range(HALF):
                            q = b * HALF + j
                            pe.wait_ge(ga.got[q], i * 16 + 16)
                            pe.wait_ge(att_in[q], i * 16 + 16)
                            for c in range(KD):
                                out = ps_m[:, b, c, j * P:(j + 1) * P]
                                nc.tensor.matmul(out, ga.rows[:, q, c * P:(c + 1) * P], g.ident[:], start=True, stop=False)
                                ins = nc.tensor.matmul(out, w[:, c * P:(c + 1) * P], att[:, q, :], start=False, stop=True)
                        ins.then_inc(made, 1)
                        pe.wait_ge(made, i * 2 + b + 1)
                        pe.sem_inc(ga.used[b], 1)
                    for b in range(2):
                        pe.wait_ge(ran, i * 4 + b * 2 + 2)
                        for k in range(2):
                            pe.wait_ge(taken, i * 4 + b * 2 + k - 1 if b * 2 + k >= 1 else i * 4)
                            for j in range(2):
                                q = k * 2 + j
                                for c in range(KD):
                                    ins = nc.tensor.transpose(ps_t[:, k, j, c * P:(c + 1) * P],
                                                              run[:, b, c, q * P:(q + 1) * P], g.ident[:])
                            ins.then_inc(turned, 1)
                        for k in range(2):
                            pe.wait_ge(taken, i * 4 + b * 2 + k + 1)
                            for j in range(2):
                                q = b * HALF + k * 2 + j
                                pe.wait_ge(sel_set, i * U + q + 1)
                                pe.wait_ge(added, i * U + (b * HALF + k * 2 - 2 if b or k else 0))
                                nc.tensor.matmul(ps_a[:, k, j, :], sel[:, q, :], back[:, q, :],
                                                 start=True, stop=True).then_inc(summed, 1)

            @block.scalar
            def _(act):
                with nc.scalar.Fori(0, STEPS // U) as i:
                    for b in range(2):
                        for k in range(2):
                            act.wait_ge(turned, i * 4 + b * 2 + k + 1)
                            act.wait_ge(summed, i * U)
                            q = b * HALF + k * 2
                            nc.scalar.activation(back[:, q:q + 2, :].rearrange("p j d -> p (j d)"),
                                                 ps_t[:, k, :, :].rearrange("p j d -> p (j d)"), ACT.Copy).then_inc(taken, 1)

            @block.vector
            def _(dve):
                v = nc.vector
                v.memset(acc[:, :, 0:D], 0.0).then_inc(zeroed, 1)
                v.memset(run[:], 0.0).then_inc(zeroed, 1)
                dve.wait_ge(zeroed, 2)
                with nc.vector.Fori(0, STEPS // U) as i:
                    tiles = [nc.vector.value_load(g.tile_row[0:1, ds(i * U + j, 1)], min_val=0, max_val=NT - 1) for j in range(U)]
                    dve.wait_ge(summed, i * U)
                    v.tensor_copy(lasts[:], g.last_a[:, ds(i * U, U)]).then_inc(lasts_in, 1)
                    dve.wait_ge(lasts_in, i + 1)
                    for j in range(U):
                        v.tensor_scalar(sel[:, j, :], g.lane[:], lasts[:, j:j + 1], None, ALU.is_equal).then_inc(sel_set, 1)
                    for b in range(2):
                        dve.wait_ge(made, i * 2 + b + 1)
                        dve.wait_ge(same_in[b], i * 16 + 16)
                        dve.wait_ge(ran, i * 4 + 2 * b)
                        dve.wait_ge(turned, i * 4)
                        for c in range(KD):
                            v.tensor_tensor_scan(run[:, b, c, :], same[:, b, :], ps_m[:, b, c, 0:HP], run[:, 1 - b, c, HP - 1:HP],
                                                 ALU.mult, ALU.max).then_inc(ran, 1)
                    for j in range(U):
                        dve.wait_ge(summed, i * U + (j | 1) + 1)
                        dve.wait_ge(added, i * U + j)
                        at = acc[:, ds(tiles[j], 1), 0:D].rearrange("p a c -> p (a c)")
                        v.tensor_tensor(at, at, ps_a[:, (j // 2) % 2, j % 2, :], ALU.add).then_inc(added, 1)


def gnn3(nc, g):
    with Phase(nc) as ph:
        sb = ph.sb
        hv = sb("hv", [P, NT, D], F32)
        acc = sb("acc", [P, NT, AC], F32)
        hw = sb("hw", [P, NT, D], F32)
        node_rows(nc, g, [g.x], [(g.ins["L3_gnn_W_in"], 0, 0)], D, g.ins["L3_gnn_b_in"], [(0, D, hv, None)], ln=True)
        for w, b in ((g.ins["L3_gnn_W_u0"], g.ins["L3_gnn_b_u0"]), (g.ins["L3_gnn_W_u1"], g.ins["L3_gnn_b_u1"])):
            node_rows(nc, g, [hv], [(w[0:D, :], 0, 0)], D, b, [(0, D, hw, g.tab)])
            edge_max(nc, g, g.tab, w[D:D + EA, :], acc)
            bulk(nc, [("v", lambda v: v.tensor_add(hv[:], hv[:], acc[:, :, 0:D]))])
        node_rows(nc, g, [hv], [(g.ins["L3_gnn_W_ro"], 0, 0)], D, g.ins["L3_gnn_b_ro"], [(0, D, g.x, None)], relu_add=True)


def ffn3(nc, g):
    H, G, C = 8, 64, 64
    M = H // 2
    HF = TOK // 2
    with Phase(nc) as ph:
        sb = ph.sb
        wt = sb("wt", [P, M, NP_], F32)
        tok = sb("tok", [P, M, P + 1], F32)
        wout = sb("wout", [C, H, D], F32)
        mix = sb("mix", [P, M, D], F32)
        with Phase(nc) as p2:
            slice_weights(nc, g, p2, wt, tok, H, G, C, M, HF)
        with Phase(nc) as p2:
            slice_attention(nc, g, p2, tok, mix, H, G, C, M)
        with Phase(nc) as p2:
            slices_out(nc, g, p2, wt, mix, M)


def slice_weights(nc, g, ph, wt, tok, H, G, C, M, HF):
    sb = ph.sb
    xt = sb("xt", [P, KD, NP_], F32)
    wfx, wx = sb("wfx", [P, KD, H * C], F32), sb("wx", [P, KD, H * C], F32)
    bfx, bx = sb("bfx", [P, H * C], F32), sb("bx", [P, M], F32)
    wsl = sb("wsl", [P, P], F32)
    bsl, rtemp = sb("bsl", [P, H, G], F32), sb("rtemp", [P, H, G], F32)
    bs_row, temp = sb("bs_row", [P, G], F32), sb("temp", [P, H], F32)
    real = sb("real", [P, NT], F32)
    node_rows(nc, g, [g.x], [], 0, None, [], ln=True, xt=xt)
    with Phase(nc) as p2:
        made, zed = p2.sem("made"), p2.sem("zed")
        with nc.Block() as block:
            @block.gpsimd
            def _(pool):
                nc.gpsimd.memset(wsl[:], 0.0).then_inc(zed, 1)
                nc.gpsimd.memset(tok[:], 0.0).then_inc(zed, 1)
                nc.gpsimd.iota(real[:], [[P, NT]], 0, 1, allow_small_or_imprecise_dtypes=True).then_inc(made, 1)
    bulk(nc, [("v", lambda v: v.tensor_scalar(real[:], real[:], float(N), None, ALU.is_lt)),
              ("v", lambda v: v.tensor_scalar(temp[:], temp[:], 0.1, 5.0, ALU.max, ALU.min)),
              ("v", lambda v: v.reciprocal(temp[:], temp[:])),
              ("v", lambda v: v.tensor_copy(rtemp[:], temp[:].unsqueeze(2).broadcast_to([P, H, G]))),
              ("v", lambda v: v.tensor_copy(bsl[:], bs_row[:].unsqueeze(1).broadcast_to([P, H, G])))],
         loads=[(wfx[:], by_partition(g.ins["L3_ffn_W_fx"])), (wx[:], by_partition(g.ins["L3_ffn_W_x"])), (bfx[:], row_bc(g.ins["L3_ffn_b_fx"])),
                (bx[:], g.ins["L3_ffn_b_x"]), (wsl[0:C, 0:G], g.ins["L3_ffn_W_slice"]), (wsl[C:P, G:P], g.ins["L3_ffn_W_slice"]),
                (bs_row[:], row_bc(g.ins["L3_ffn_b_slice"])), (temp[:], row_bc(g.ins["L3_ffn_temperature"]))])
    with Phase(nc) as p2:
        sb, ps, sem = p2.sb, p2.ps, p2.sem
        xc = sb("xc", [P, KD, TOK], F32)
        xm = sb("xm", [P, M, TOK], F32)
        z = sb("z", [P, 2, H, G], F32)
        w = sb("w", [P, CH, H, G], F32)
        fx = sb("fx", [P, CH, M, P + 1], F32)
        top, tot = sb("top", [P, 2, H], F32), sb("tot", [P, 2, H], F32)
        rc = sb("rc", [P, CH], F32)
        ps_x = ps("ps_x", [P, 2, 512])
        ps_l = ps("ps_l", [P, 2, 512])
        ps_f = ps("ps_f", [P, 1, 512])
        ps_t = ps("ps_t", [P, 1, 512])
        ps_s = ps("ps_s", [P, 2, 512])
        ones, xc_in, mid, midded, lmade, lread, zset, eset, wset, fmade, fset, tmade, ttaken, smade, sread, own = (
            sem(x) for x in ("ones", "xc_in", "mid", "midded", "lmade", "lread", "zset", "eset", "wset", "fmade", "fset",
                             "tmade", "ttaken", "smade", "sread", "own"))
        with nc.Block() as block:
            @block.tensor
            def _(pe):
                with nc.tensor.Fori(0, NT // CH) as i:
                    pe.wait_ge(xc_in, i + 1)
                    for n in range(2 * M):
                        m, h = n // 2, n % 2
                        pe.wait_ge(midded, i * 2 * M + max(n - 1, 0))
                        for k in range(KD):
                            ins = nc.tensor.matmul(ps_x[:, n % 2, 0:HF], wx[:, k, m * P:(m + 1) * P], xc[:, k, h * HF:(h + 1) * HF],
                                                   start=k == 0, stop=k == KD - 1)
                        ins.then_inc(mid, 1)
                    pe.wait_ge(midded, i * 2 * M + 2 * M)

                    def first(t):
                        pe.wait_ge(lread, i * CH + max(t - 1, 0))
                        for m in range(M):
                            ins = nc.tensor.matmul(ps_l[:, t % 2, m * P:(m + 1) * P], xm[:, m, t * P:(t + 1) * P], wsl[:],
                                                   start=True, stop=True)
                        ins.then_inc(lmade, 1)
                        pe.wait_ge(fset, i * CH + t)
                        for k in range(KD):
                            ins = nc.tensor.matmul(ps_f[:, 0, :], xc[:, k, t * P:(t + 1) * P], wfx[:, k, :],
                                                   start=k == 0, stop=k == KD - 1)
                        ins.then_inc(fmade, 1)

                    def second(t):
                        pe.wait_ge(wset, i * CH + t + 1)
                        pe.wait_ge(ttaken, i * CH + t)
                        for m in range(M):
                            ins = nc.tensor.transpose(ps_t[:, 0, m * P:(m + 1) * P],
                                                      w[:, t, 2 * m:2 * m + 2, :].rearrange("p h g -> p (h g)"), g.ident[:])
                        ins.then_inc(tmade, 1)
                        pe.wait_ge(fset, i * CH + t + 1)
                        pe.wait_ge(sread, i * CH + t)
                        for m in range(M):
                            ins = nc.tensor.matmul(ps_s[:, m // 2, (m % 2) * (P + 1):(m % 2 + 1) * (P + 1)],
                                                   w[:, t, 2 * m:2 * m + 2, :].rearrange("p h g -> p (h g)"), fx[:, t, m, :],
                                                   start=True, stop=True)
                        ins.then_inc(smade, 1)

                    first(0)
                    for t in range(CH):
                        if t + 1 < CH:
                            first(t + 1)
                        second(t)

            @block.scalar
            def _(act):
                a = nc.scalar
                with nc.scalar.Fori(0, NT // CH) as i:
                    act.wait_ge(fmade, i * CH)
                    a.activation(xc[:], xt[:, :, ds(i * TOK, TOK)], ACT.Copy).then_inc(xc_in, 1)
                    for n in range(2 * M):
                        m, h = n // 2, n % 2
                        act.wait_ge(mid, i * 2 * M + n + 1)
                        act.wait_ge(lmade, i * CH)
                        a.activation(xm[:, m, h * HF:(h + 1) * HF], ps_x[:, n % 2, 0:HF], ACT.Identity,
                                     bias=bx[:, m:m + 1]).then_inc(midded, 1)
                    for t in range(CH):
                        act.wait_ge(zset, i * CH + t + 1)
                        a.activation(z[:, t % 2, :, :], z[:, t % 2, :, :], ACT.Exp).then_inc(eset, 1)
                        if t:
                            act.wait_ge(tmade, i * CH + t)
                            a.activation(wt[:, :, ds((i * CH + t - 1) * P, P)],
                                         ps_t[:, 0, :].rearrange("p (m n) -> p m n", m=M), ACT.Copy).then_inc(ttaken, 1)
                    act.wait_ge(tmade, i * CH + CH)
                    a.activation(wt[:, :, ds((i * CH + CH - 1) * P, P)],
                                 ps_t[:, 0, :].rearrange("p (m n) -> p m n", m=M), ACT.Copy).then_inc(ttaken, 1)

            @block.vector
            def _(dve):
                v = nc.vector
                v.memset(fx[:], 1.0).then_inc(ones, 1)
                dve.wait_ge(ones, 1)
                per = CH * 7 + 1
                with nc.vector.Fori(0, NT // CH) as i:
                    o = Order(dve, own, i * per)
                    o.link(v.tensor_copy(rc[:], real[:, ds(i * CH, CH)]))

                    def before(t):
                        b = t % 2
                        zb, tb = z[:, b, :, :], top[:, b, :]
                        dve.wait_ge(lmade, i * CH + t + 1)
                        v.tensor_tensor(zb, ps_l[:, b, :].rearrange("p (h g) -> p h g", h=H), bsl[:], ALU.add).then_inc(lread, 1)
                        dve.wait_ge(lread, i * CH + t + 1)
                        o.link(v.tensor_tensor(zb, zb, rtemp[:], ALU.mult))
                        o.link(v.tensor_reduce(tb, zb, AX_X, ALU.max))
                        v.tensor_tensor(zb, zb, tb.unsqueeze(2).broadcast_to([P, H, G]), ALU.subtract).then_inc(zset, 1)
                        dve.wait_ge(fmade, i * CH + t + 1)
                        dve.wait_ge(smade, i * CH)
                        v.tensor_tensor(fx[:, t, :, 0:P], ps_f[:, 0, :].rearrange("p (m c) -> p m c", m=M),
                                        bfx[:].rearrange("p (m c) -> p m c", m=M), ALU.add).then_inc(fset, 1)

                    def behind(t):
                        b = t % 2
                        zb, sb_ = z[:, b, :, :], tot[:, b, :]
                        dve.wait_ge(eset, i * CH + t + 1)
                        o.link(v.tensor_reduce(sb_, zb, AX_X, ALU.add))
                        o.link(v.reciprocal(sb_, sb_))
                        o.link(v.tensor_scalar(sb_, sb_, rc[:, t:t + 1], None, ALU.mult))
                        dve.wait_ge(smade, i * CH)
                        v.tensor_tensor(w[:, t, :, :], zb, sb_.unsqueeze(2).broadcast_to([P, H, G]), ALU.mult).then_inc(wset, 1)
                        dve.wait_ge(wset, i * CH + t + 1)
                        dve.wait_ge(smade, i * CH + t + 1)
                        for q in range(2):
                            o.link(v.tensor_tensor(tok[:, 2 * q:2 * q + 2, :], tok[:, 2 * q:2 * q + 2, :],
                                                   ps_s[:, q, 0:2 * (P + 1)].rearrange("p (m c) -> p m c", m=2), ALU.add))
                        dve.sem_inc(sread, 1)

                    before(0)
                    for t in range(CH):
                        if t + 1 < CH:
                            before(t + 1)
                        behind(t)


def slice_attention(nc, g, ph, tok, mix, H, G, C, M):
    sb, ps, sem = ph.sb, ph.ps, ph.sem
    wq, wk, wv = (sb(n, [C, C], F32) for n in ("wq", "wk", "wv"))
    wout = sb("wout", [C, H, D], F32)
    rn = sb("rn", [P, M], F32)
    st = sb("st", [P, M, C], F32)
    stt = sb("stt", [C, H, G], F32)
    qt, kt = sb("qt", [C, H, G], F32), sb("kt", [C, H, G], F32)
    vv = sb("vv", [G, H, C], F32)
    at = sb("at", [G, H, G], F32)
    att = sb("att", [G, H, G], F32)
    top, tot = sb("top", [G, H], F32), sb("tot", [G, H], F32)
    ost = sb("ost", [C, H, P], F32)
    pss = [ps(f"ps{n}", [P, 512]) for n in range(8)]
    w_in, own, pe_own = sem("w_in"), sem("own"), sem("pe_own")
    flat = lambda a: a.rearrange("p h g -> p (h g)")
    with nc.Block() as block:
        @block.sync
        def _(sp):
            for t, s_ in ((wq[:], g.ins["L3_ffn_W_q"]), (wk[:], g.ins["L3_ffn_W_k"]), (wv[:], g.ins["L3_ffn_W_v"]),
                          (wout[:], g.ins["L3_ffn_W_out"].rearrange("(h c) d -> c h d", c=C))):
                sp.dma_start(t, s_).then_inc(w_in, 16)
            sp.wait_ge(w_in, 64)

        @block.vector
        def _(dve):
            v = nc.vector
            o = Order(dve, own)
            o.link(v.memset(ost[:], 0.0))
            o.link(v.tensor_scalar(rn[:], tok[:, :, P], 1e-5, None, ALU.add))
            o.link(v.reciprocal(rn[:], rn[:]))
            for h in range(2):
                p = slice(h * G, (h + 1) * G)
                o.link(v.tensor_tensor(st[p, :, :], tok[p, :, h * C:(h + 1) * C],
                                       rn[p, :].unsqueeze(2).broadcast_to([G, M, C]), ALU.mult))
            dve.wait_ge(pe_own, 1)
            o.link(v.tensor_copy(flat(stt[:]), pss[0][0:C, :]))
            dve.wait_ge(pe_own, 2)
            o.link(v.tensor_copy(flat(qt[:]), pss[1][0:C, :]))
            o.link(v.tensor_copy(flat(kt[:]), pss[2][0:C, :]))
            o.link(v.tensor_copy(flat(vv[:]), pss[3][0:G, :]))
            dve.wait_ge(pe_own, 3)
            o.link(v.tensor_scalar(flat(at[:]), pss[4][0:G, :], C ** -0.5, None, ALU.mult))
            o.link(v.tensor_reduce(top[:], at[:], AX_X, ALU.max))
            o.link(v.tensor_tensor(at[:], at[:], top[:].unsqueeze(2).broadcast_to([G, H, G]), ALU.subtract))
            n_exp = o.at
            dve.wait_ge(own, n_exp + 1)
            o.at = n_exp + 1
            o.link(v.tensor_reduce(tot[:], at[:], AX_X, ALU.add))
            o.link(v.reciprocal(tot[:], tot[:]))
            o.link(v.tensor_tensor(at[:], at[:], tot[:].unsqueeze(2).broadcast_to([G, H, G]), ALU.mult))
            dve.wait_ge(pe_own, 4)
            o.link(v.tensor_copy(flat(att[:]), pss[5][0:G, :]))
            dve.wait_ge(pe_own, 5)
            for h in range(2):
                o.link(v.tensor_copy(ost[:, h::2, h * G:(h + 1) * G],
                                     pss[6][0:C, :].rearrange("p (h g) -> p h g", h=H)[:, h::2, :]))
            dve.wait_ge(pe_own, 6)
            for q in range(2):
                o.link(v.tensor_copy(mix[:, 2 * q:2 * q + 2, :].rearrange("p m d -> p (m d)"), pss[7 * q][:, :]))

        @block.scalar
        def _(act):
            act.wait_ge(own, 12)
            nc.scalar.activation(at[:], at[:], ACT.Exp).then_inc(own, 1)

        @block.tensor
        def _(pe):
            t = nc.tensor
            pe.wait_ge(own, 5)
            for m in range(M):
                ins = t.transpose(pss[0][0:C, m * P:(m + 1) * P], st[:, m, :], g.ident[:])
            ins.then_inc(pe_own, 1)
            pe.wait_ge(own, 6)
            pe.wait_ge(w_in, 64)
            t.matmul(pss[1][0:C, :], wq[:], flat(stt[:]), start=True, stop=True)
            t.matmul(pss[2][0:C, :], wk[:], flat(stt[:]), start=True, stop=True)
            for h in range(H):
                ins = t.matmul(pss[3][0:G, h * C:(h + 1) * C], stt[:, h, :], wv[:], start=True, stop=True)
            ins.then_inc(pe_own, 1)
            pe.wait_ge(own, 9)
            for h in range(H):
                ins = t.matmul(pss[4][0:G, h * G:(h + 1) * G], qt[:, h, :], kt[:, h, :], start=True, stop=True)
            ins.then_inc(pe_own, 1)
            pe.wait_ge(own, 16)
            for h in range(H):
                ins = t.transpose(pss[5][0:G, h * G:(h + 1) * G], at[:, h, :], g.ident[0:G, 0:G])
            ins.then_inc(pe_own, 1)
            pe.wait_ge(own, 17)
            for h in range(H):
                ins = t.matmul(pss[6][0:C, h * G:(h + 1) * G], vv[:, h, :], att[:, h, :], start=True, stop=True)
            ins.then_inc(pe_own, 1)
            pe.wait_ge(own, 19)
            for m in range(M):
                out = pss[7 * (m // 2)][:, (m % 2) * D:(m % 2 + 1) * D]
                t.matmul(out, ost[:, 2 * m, :], wout[:, 2 * m, :], start=True, stop=False)
                ins = t.matmul(out, ost[:, 2 * m + 1, :], wout[:, 2 * m + 1, :], start=False, stop=True)
            ins.then_inc(pe_own, 1)


def slices_out(nc, g, ph, wt, mix, M):
    sb, ps, sem = ph.sb, ph.ps, ph.sem
    wc = sb("wc", [P, M, TOK], F32)
    bias = sb("bias", [P, D], F32)
    ps_o = ps("ps_o", [P, 4, 512])
    b_in, laid, made, added, biased = (sem(x) for x in ("b_in", "laid", "made", "added", "biased"))
    with nc.Block() as block:
        @block.sync
        def _(sp):
            sp.dma_start(bias[:], row_bc(g.ins["L3_ffn_b_out"])).then_inc(b_in, 16)
            sp.wait_ge(b_in, 16)

        @block.scalar
        def _(act):
            with nc.scalar.Fori(0, NT // CH) as i:
                act.wait_ge(made, i * CH)
                nc.scalar.activation(wc[:], wt[:, :, ds(i * TOK, TOK)], ACT.Copy).then_inc(laid, 1)

        @block.tensor
        def _(pe):
            with nc.tensor.Fori(0, NT // CH) as i:
                pe.wait_ge(laid, i + 1)
                for t in range(CH):
                    pe.wait_ge(added, i * CH + max(t - 3, 0))
                    for m in range(M):
                        ins = nc.tensor.matmul(ps_o[:, t % 4, 0:D], wc[:, m, t * P:(t + 1) * P], mix[:, m, :],
                                               start=m == 0, stop=m == M - 1)
                    ins.then_inc(made, 1)

        @block.vector
        def _(dve):
            v = nc.vector
            dve.wait_ge(b_in, 16)
            v.tensor_tensor(g.x[:], g.x[:], bias[:].unsqueeze(1).broadcast_to([P, NT, D]), ALU.add).then_inc(biased, 1)
            dve.wait_ge(biased, 1)
            with nc.vector.Fori(0, NT // CH) as i:
                for t in range(CH):
                    dve.wait_ge(made, i * CH + t + 1)
                    xs = g.x[:, ds(i * CH + t, 1), :].rearrange("p a d -> p (a d)")
                    v.tensor_tensor(xs, xs, ps_o[:, t % 4, 0:D], ALU.add).then_inc(added, 1)


STAGES = [gnn0, ffn0, gnn1, ffn1, gnn2, ffn2, gnn3, ffn3]


def build(nc, ins, out, first=0, last=8):
    g = Net()
    g.ins = ins

    def dram(name, shape, dt=F32):
        return nc.dram_tensor(name, shape, dt, kind="Internal").ap()

    with ExitStack() as ctx:
        def sb(name, shape, dt=F32):
            return ctx.enter_context(nc.sbuf_tensor(name, shape, dt))

        g.row_dram = dram("row_dram", [STEPS], I32)
        g.tile_dram = dram("tile_dram", [STEPS], I32)
        g.dst_slots = dram("dst_slots", [SLOTS + 1])
        g.loc_slots = dram("loc_slots", [SLOTS], BF16)
        g.same_slots = dram("same_slots", [SLOTS], BF16)
        g.seg_dram = dram("seg_dram", [4, STEPS * 8])
        g.tab = dram("tab", [NP_, D])
        g.tab2 = dram("tab2", [NP_, D])
        g.tab8 = dram("tab8", [NP_, 8])
        g.tab4 = dram("tab4", [NP_, 4])
        g.ident = sb("ident", [P, P])
        g.identb = sb("identb", [P, P], BF16)
        g.lane = sb("lane", [P, P])
        g.pidx = sb("pidx", [P, 1])
        g.row_row = sb("row_row", [1, STEPS], I32)
        g.tile_row = sb("tile_row", [1, STEPS], I32)
        g.row_b = sb("row_b", [SPG, GROUPS], I32)
        g.node0_b = sb("node0_b", [SPG, GROUPS])
        g.src_a = sb("src_a", [P, STEPS], I32)
        g.dst_a = sb("dst_a", [P, STEPS])
        g.loc_a = sb("loc_a", [P, STEPS])
        g.last_a = sb("last_a", [P, STEPS])
        g.x = sb("x", [P, NT, D])
        edge_steps(nc, g)
        slot_tables(nc, g)
        with Phase(nc) as ph:
            xin = ph.sem("xin")
            with nc.Block() as block:
                @block.sync
                def _(sp):
                    sp.dma_start(g.x[:], tile_rows(g.ins["x_in"])).then_inc(xin, 16)
                    sp.wait_ge(xin, 16)
        for stage in STAGES[first:last]:
            stage(nc, g)
        to_dram(nc, [(tile_rows(out), g.x[:])])


def layout(x):
    ap = {}
    src, dst = np.asarray(x["src"]), np.asarray(x["dst"])
    pad = EP - E
    dst_p = np.pad(dst, (0, pad), constant_values=1 << 20)
    nxt = np.pad(dst[1:], (0, pad + 1), constant_values=1 << 20)
    ap["ids"] = np.stack([np.pad(src, (0, pad)).reshape(ROWS, P), dst_p.reshape(ROWS, P), nxt.reshape(ROWS, P)],
                         1).reshape(ROWS, 3 * P)
    ap["dst_grid"] = dst.reshape(ER, EC)
    ap["attr_t"] = np.pad(np.asarray(x["edge_attr_64"]), ((0, pad), (0, 0))).reshape(ROWS, P, EA).transpose(0, 2, 1)
    ap["x_in"] = np.pad(np.asarray(x["x"]), ((0, NP_ - N), (0, 0)))
    for k, a in x.items():
        if k in ("x", "src", "dst", "edge_attr_64"):
            continue
        a = np.asarray(a)
        if k.startswith("L0_gnn") and a.shape == (8, 32):
            a = a.reshape(D)
        ap[k] = a

    def on_partitions(a):
        return a.reshape(NE, -1, P).transpose(2, 0, 1)

    ap["L1_gnn_b"] = np.concatenate([ap.pop(f"L1_gnn_b{n}") for n in "qkvs"])
    ap["L1_gnn_alpha_res"] = ap["L1_gnn_alpha_res"].reshape(1)
    for k in ("L1_gnn_gamma", "L1_gnn_beta", "L2_gnn_att_src", "L2_gnn_att_dst", "L3_ffn_temperature"):
        ap[k] = ap[k].reshape(-1)
    ap["L1_ffn_b1"], ap["L2_ffn_b1"] = on_partitions(ap["L1_ffn_b1"]), on_partitions(ap["L2_ffn_b1"])
    ap["L2_ffn_router_w"] = ap["L2_ffn_router_w"].T
    ap["L3_ffn_b_x"] = ap["L3_ffn_b_x"].reshape(-1, P).T
    for q in "12":
        ap[f"L0_ffn_vec{q}"] = np.stack([on_partitions(ap.pop(f"L0_ffn_{n}{q}")) for n in ("b", "g", "be", "m", "v")], 1)
    return {k: np.ascontiguousarray(a) for k, a in ap.items()}


def kernel(**inputs):
    import concourse.bacc as bacc
    from concourse.bass_utils import run_bass_kernel_spmd

    nc = bacc.Bacc("TRN2", target_bir_lowering=False, num_devices=1)
    arrays = {f"in_{k}": a for k, a in layout(inputs).items()}
    ins = {k[3:]: nc.dram_tensor(k, a.shape, mybir.dt.from_np(a.dtype), kind="ExternalInput").ap()
           for k, a in arrays.items()}
    out = nc.dram_tensor("out_x", [NP_, D], F32, kind="ExternalOutput").ap()
    build(nc, ins, out)
    r = run_bass_kernel_spmd(nc, [arrays], core_ids=[0])
    return r.results[0]["out_x"][0:N]
```
